# Optimizing a Trainium2 kernel written in Bass

```python
import numpy as np
import jax
import jax.numpy as jnp

def _softmax(x, axis=-1):
    return jax.nn.softmax(x, axis=axis)

def _gelu(x):
    return jax.nn.gelu(x, approximate=True)

def _silu(x):
    return jax.nn.silu(x)

def _sigmoid(x):
    return jax.nn.sigmoid(x)

def _layernorm(x, axis=-1, eps=1e-05):
    m = jnp.mean(x, axis=axis, keepdims=True)
    v = jnp.var(x, axis=axis, keepdims=True)
    return (x - m) / jnp.sqrt(v + eps)

def _scatter_add(tgt, idx, src, axis=0):
    return tgt.at[idx].add(src)

def _segment_sum(src, seg, n):
    return jax.ops.segment_sum(src, seg, n)
kernel_name = 'mk_prb_d1_jaxref_r8_7fb352'

def setup_inputs(seed: int=0):
    np.random.seed(seed)
    _w = jnp.asarray

    def _L0_attn_setup():
        import jax, jax.numpy as jnp
        import numpy as np
        HIDDEN = 128
        HEAD_DIM = 64
        N_HEADS = HIDDEN // HEAD_DIM
        BATCH = 2
        SEQ = 256
        ROT_DIM = HEAD_DIM // 2
        THETA = 10000.0
        SCALE_BASE = 512.0
        EPS = 1e-05

        def _layernorm(x, w, b):
            m = jnp.mean(x, axis=-1, keepdims=True)
            v = jnp.mean(jnp.square(x - m), axis=-1, keepdims=True)
            return (x - m) * jax.lax.rsqrt(v + EPS) * w + b

        def _rotate_half(x):
            xs = x.reshape(x.shape[:-1] + (ROT_DIM // 2, 2))
            x1, x2 = (xs[..., 0], xs[..., 1])
            return jnp.stack((-x2, x1), axis=-1).reshape(x.shape)

        def _xpos_rotary(q, k):
            S = q.shape[-2]
            half = jnp.arange(0, ROT_DIM, 2, dtype=jnp.float32)
            inv_freq = 1.0 / THETA ** (half / ROT_DIM)
            t = jnp.arange(S, dtype=jnp.float32)
            freqs = jnp.repeat(t[:, None] * inv_freq, 2, axis=-1)
            scale_vals = (half + 0.4 * ROT_DIM) / (1.4 * ROT_DIM)
            power = (t - S // 2) / SCALE_BASE
            scale = scale_vals[None, :] ** power[:, None]
            scale = jnp.concatenate((scale, scale), axis=-1)
            cos, sin = (jnp.cos(freqs), jnp.sin(freqs))

            def apply(x, sc):
                xl, xr = (x[..., :ROT_DIM], x[..., ROT_DIM:])
                xl = xl * cos * sc + _rotate_half(xl) * sin * sc
                return jnp.concatenate((xl, xr), axis=-1)
            return (apply(q, scale), apply(k, 1.0 / scale))

        def _mish(x):
            return x * jnp.tanh(jax.nn.softplus(x))
        key = jax.random.key(seed)
        ks = jax.random.split(key, 8)

        def lin(k, shape, fan_in):
            b = 1.0 / np.sqrt(fan_in)
            return jax.random.uniform(k, shape, jnp.float32, -b, b)
        return {'x': jax.random.normal(ks[0], (BATCH, SEQ, HIDDEN), jnp.float32), 'ln1_w': jnp.ones((HIDDEN,), jnp.float32), 'ln1_b': jnp.zeros((HIDDEN,), jnp.float32), 'wqkv_w': lin(ks[1], (HIDDEN, 3 * HIDDEN), HIDDEN), 'wg_w': lin(ks[2], (HIDDEN, HIDDEN), HIDDEN), 'wo_w': lin(ks[3], (HIDDEN, HIDDEN), HIDDEN), 'gn_w': jnp.ones((N_HEADS,), jnp.float32), 'gn_b': jnp.zeros((N_HEADS,), jnp.float32), 'ln2_w': jnp.ones((HIDDEN,), jnp.float32), 'ln2_b': jnp.zeros((HIDDEN,), jnp.float32), 'w1_w': lin(ks[4], (HIDDEN, HIDDEN), HIDDEN), 'w1_b': lin(ks[5], (HIDDEN,), HIDDEN), 'w2_w': lin(ks[6], (HIDDEN, HIDDEN), HIDDEN), 'w2_b': lin(ks[7], (HIDDEN,), HIDDEN)}
    _L0_attn_in = _L0_attn_setup()

    def _L0_ffn_setup():
        import jax, jax.numpy as jnp
        import numpy as np
        import math
        N_EMBD = 128
        HIDDEN = 4 * N_EMBD
        N_EXPERTS = 8
        TOP_K = 2
        B, T = (4, 256)

        def new_gelu(x):
            c = math.sqrt(2.0 / math.pi)
            return 0.5 * x * (1.0 + jnp.tanh(c * (x + 0.044715 * x * x * x)))

        def _moe_forward(x, Wfc_s, bfc_s, Wproj_s, bproj_s, Wr, Wfc, bfc, Wproj, bproj):
            Bb, Tt, C = x.shape
            xf = x.reshape(Bb * Tt, C)
            N = Bb * Tt
            shared = new_gelu(xf @ Wfc_s + bfc_s) @ Wproj_s + bproj_s
            logits = xf @ Wr
            probs = jax.nn.softmax(logits, axis=-1)
            topk_p, topk_i = jax.lax.top_k(probs, TOP_K)
            topk_p = topk_p / jnp.sum(topk_p, axis=-1, keepdims=True)
            gate = jnp.zeros((N, N_EXPERTS), dtype=xf.dtype)
            gate = gate.at[jnp.arange(N)[:, None], topk_i].add(topk_p)
            routed = jnp.zeros_like(xf)
            for e in range(N_EXPERTS):
                h = new_gelu(xf @ Wfc[e] + bfc[e]) @ Wproj[e] + bproj[e]
                routed = routed + h * gate[:, e:e + 1]
            return (shared + routed).reshape(Bb, Tt, C)
        key = jax.random.key(seed)
        ks = jax.random.split(key, 10)
        s = 0.02
        return {'x': jax.random.normal(ks[0], (B, T, N_EMBD), dtype=jnp.float32), 'Wfc_s': jax.random.normal(ks[1], (N_EMBD, HIDDEN), dtype=jnp.float32) * s, 'bfc_s': jnp.zeros((HIDDEN,), dtype=jnp.float32), 'Wproj_s': jax.random.normal(ks[2], (HIDDEN, N_EMBD), dtype=jnp.float32) * s, 'bproj_s': jnp.zeros((N_EMBD,), dtype=jnp.float32), 'Wr': jax.random.normal(ks[3], (N_EMBD, N_EXPERTS), dtype=jnp.float32) * s, 'Wfc': jax.random.normal(ks[4], (N_EXPERTS, N_EMBD, HIDDEN), dtype=jnp.float32) * s, 'bfc': jnp.zeros((N_EXPERTS, HIDDEN), dtype=jnp.float32), 'Wproj': jax.random.normal(ks[5], (N_EXPERTS, HIDDEN, N_EMBD), dtype=jnp.float32) * s, 'bproj': jnp.zeros((N_EXPERTS, N_EMBD), dtype=jnp.float32)}
    _L0_ffn_in = _L0_ffn_setup()
    _d = {'L0_attn_x': _L0_attn_in['x'], 'L0_attn_ln1_w': _L0_attn_in['ln1_w'], 'L0_attn_ln1_b': _L0_attn_in['ln1_b'], 'L0_attn_wqkv_w': _L0_attn_in['wqkv_w'], 'L0_attn_wg_w': _L0_attn_in['wg_w'], 'L0_attn_wo_w': _L0_attn_in['wo_w'], 'L0_attn_gn_w': _L0_attn_in['gn_w'], 'L0_attn_gn_b': _L0_attn_in['gn_b'], 'L0_attn_ln2_w': _L0_attn_in['ln2_w'], 'L0_attn_ln2_b': _L0_attn_in['ln2_b'], 'L0_attn_w1_w': _L0_attn_in['w1_w'], 'L0_attn_w1_b': _L0_attn_in['w1_b'], 'L0_attn_w2_w': _L0_attn_in['w2_w'], 'L0_attn_w2_b': _L0_attn_in['w2_b'], 'L0_ffn_Wfc_s': _L0_ffn_in['Wfc_s'], 'L0_ffn_bfc_s': _L0_ffn_in['bfc_s'], 'L0_ffn_Wproj_s': _L0_ffn_in['Wproj_s'], 'L0_ffn_bproj_s': _L0_ffn_in['bproj_s'], 'L0_ffn_Wr': _L0_ffn_in['Wr'], 'L0_ffn_Wfc': _L0_ffn_in['Wfc'], 'L0_ffn_bfc': _L0_ffn_in['bfc'], 'L0_ffn_Wproj': _L0_ffn_in['Wproj'], 'L0_ffn_bproj': _L0_ffn_in['bproj']}
    _x0 = _d['L0_attn_x']
    _d['L0_attn_x'] = jax.random.normal(jax.random.fold_in(jax.random.key(seed), 1), (4, 1024, 128), dtype=_x0.dtype)
    del _x0
    return _d

def reference(L0_attn_x, L0_attn_ln1_w, L0_attn_ln1_b, L0_attn_wqkv_w, L0_attn_wg_w, L0_attn_wo_w, L0_attn_gn_w, L0_attn_gn_b, L0_attn_ln2_w, L0_attn_ln2_b, L0_attn_w1_w, L0_attn_w1_b, L0_attn_w2_w, L0_attn_w2_b, L0_ffn_Wfc_s, L0_ffn_bfc_s, L0_ffn_Wproj_s, L0_ffn_bproj_s, L0_ffn_Wr, L0_ffn_Wfc, L0_ffn_bfc, L0_ffn_Wproj, L0_ffn_bproj):

    def _L0_attn_ref(x, ln1_w, ln1_b, wqkv_w, wg_w, wo_w, gn_w, gn_b, ln2_w, ln2_b, w1_w, w1_b, w2_w, w2_b):
        import jax, jax.numpy as jnp
        import numpy as np
        HIDDEN = 128
        HEAD_DIM = 64
        N_HEADS = HIDDEN // HEAD_DIM
        BATCH = 2
        SEQ = 256
        ROT_DIM = HEAD_DIM // 2
        THETA = 10000.0
        SCALE_BASE = 512.0
        EPS = 1e-05

        def _layernorm(x, w, b):
            m = jnp.mean(x, axis=-1, keepdims=True)
            v = jnp.mean(jnp.square(x - m), axis=-1, keepdims=True)
            return (x - m) * jax.lax.rsqrt(v + EPS) * w + b

        def _rotate_half(x):
            xs = x.reshape(x.shape[:-1] + (ROT_DIM // 2, 2))
            x1, x2 = (xs[..., 0], xs[..., 1])
            return jnp.stack((-x2, x1), axis=-1).reshape(x.shape)

        def _xpos_rotary(q, k):
            S = q.shape[-2]
            half = jnp.arange(0, ROT_DIM, 2, dtype=jnp.float32)
            inv_freq = 1.0 / THETA ** (half / ROT_DIM)
            t = jnp.arange(S, dtype=jnp.float32)
            freqs = jnp.repeat(t[:, None] * inv_freq, 2, axis=-1)
            scale_vals = (half + 0.4 * ROT_DIM) / (1.4 * ROT_DIM)
            power = (t - S // 2) / SCALE_BASE
            scale = scale_vals[None, :] ** power[:, None]
            scale = jnp.concatenate((scale, scale), axis=-1)
            cos, sin = (jnp.cos(freqs), jnp.sin(freqs))

            def apply(x, sc):
                xl, xr = (x[..., :ROT_DIM], x[..., ROT_DIM:])
                xl = xl * cos * sc + _rotate_half(xl) * sin * sc
                return jnp.concatenate((xl, xr), axis=-1)
            return (apply(q, scale), apply(k, 1.0 / scale))

        def _mish(x):
            return x * jnp.tanh(jax.nn.softplus(x))
        B, S, _ = x.shape
        h = _layernorm(x, ln1_w, ln1_b)
        qkv = (h @ wqkv_w).reshape(B, S, N_HEADS, 3 * HEAD_DIM).transpose(0, 2, 1, 3)
        q, k, v = jnp.split(qkv, 3, axis=-1)
        q, k = _xpos_rotary(q, k)
        gamma = 1.0 - 2.0 ** (-5.0 - jnp.arange(N_HEADS, dtype=jnp.float32))
        idx = jnp.arange(S)
        nm = (idx[:, None] - idx[None, :]).astype(jnp.float32)
        decay = jnp.where(nm >= 0, gamma[:, None, None] ** nm, 0.0)
        ret = jnp.einsum('bhsd,bhtd->bhst', q, k) * decay[None]
        ret = jnp.einsum('bhst,bhtd->bhsd', ret, v)
        m = jnp.mean(ret, axis=(2, 3), keepdims=True)
        va = jnp.mean(jnp.square(ret - m), axis=(2, 3), keepdims=True)
        ret = (ret - m) * jax.lax.rsqrt(va + EPS)
        ret = ret * gn_w[None, :, None, None] + gn_b[None, :, None, None]
        y = ret.transpose(0, 2, 1, 3).reshape(B, S, HIDDEN)
        y = _mish(h @ wg_w) * y
        y = y @ wo_w
        y = y + x
        z = _layernorm(y, ln2_w, ln2_b)
        ffn = jax.nn.gelu(z @ w1_w + w1_b, approximate=False) @ w2_w + w2_b
        return ffn + y

    def _L0_ffn_ref(x, Wfc_s, bfc_s, Wproj_s, bproj_s, Wr, Wfc, bfc, Wproj, bproj):
        import jax, jax.numpy as jnp
        import numpy as np
        import math
        N_EMBD = 128
        HIDDEN = 4 * N_EMBD
        N_EXPERTS = 8
        TOP_K = 2
        B, T = (4, 256)

        def new_gelu(x):
            c = math.sqrt(2.0 / math.pi)
            return 0.5 * x * (1.0 + jnp.tanh(c * (x + 0.044715 * x * x * x)))

        def _moe_forward(x, Wfc_s, bfc_s, Wproj_s, bproj_s, Wr, Wfc, bfc, Wproj, bproj):
            Bb, Tt, C = x.shape
            xf = x.reshape(Bb * Tt, C)
            N = Bb * Tt
            shared = new_gelu(xf @ Wfc_s + bfc_s) @ Wproj_s + bproj_s
            logits = xf @ Wr
            probs = jax.nn.softmax(logits, axis=-1)
            topk_p, topk_i = jax.lax.top_k(probs, TOP_K)
            topk_p = topk_p / jnp.sum(topk_p, axis=-1, keepdims=True)
            gate = jnp.zeros((N, N_EXPERTS), dtype=xf.dtype)
            gate = gate.at[jnp.arange(N)[:, None], topk_i].add(topk_p)
            routed = jnp.zeros_like(xf)
            for e in range(N_EXPERTS):
                h = new_gelu(xf @ Wfc[e] + bfc[e]) @ Wproj[e] + bproj[e]
                routed = routed + h * gate[:, e:e + 1]
            return (shared + routed).reshape(Bb, Tt, C)
        return _moe_forward(x, Wfc_s, bfc_s, Wproj_s, bproj_s, Wr, Wfc, bfc, Wproj, bproj)
    x = L0_attn_x
    xn = _layernorm(x, axis=-1)
    x = x + _L0_attn_ref(xn, L0_attn_ln1_w, L0_attn_ln1_b, L0_attn_wqkv_w, L0_attn_wg_w, L0_attn_wo_w, L0_attn_gn_w, L0_attn_gn_b, L0_attn_ln2_w, L0_attn_ln2_b, L0_attn_w1_w, L0_attn_w1_b, L0_attn_w2_w, L0_attn_w2_b) + _L0_ffn_ref(xn, L0_ffn_Wfc_s, L0_ffn_bfc_s, L0_ffn_Wproj_s, L0_ffn_bproj_s, L0_ffn_Wr, L0_ffn_Wfc, L0_ffn_bfc, L0_ffn_Wproj, L0_ffn_bproj)
    return x

_drawn_inputs = setup_inputs


def setup_inputs(seed=0):
    import zlib

    import numpy as np

    out = dict(_drawn_inputs(seed))
    spreads = {'L0_attn_ln1_w': (1.0, 0.2),
     'L0_attn_ln1_b': (0.0, 0.41),
     'L0_attn_gn_w': (1.0, 0.6),
     'L0_attn_gn_b': (0.0, 0.8),
     'L0_attn_ln2_w': (1.0, 0.6),
     'L0_attn_ln2_b': (0.0, 0.669),
     'L0_ffn_bfc_s': (0.0, 0.615),
     'L0_ffn_bproj_s': (0.0, 0.1),
     'L0_ffn_bfc': (0.0, 0.8),
     'L0_ffn_bproj': (0.0, 0.1)}
    factors = {'L0_attn_w1_b': 5.541, 'L0_ffn_Wfc': 3.027, 'L0_ffn_Wproj': 2.744}
    for name, (base, spread) in spreads.items():
        noise = np.random.default_rng([zlib.crc32(name.encode()), seed]).standard_normal(out[name].shape)
        drawn = base * np.exp(spread * noise) if base else spread * noise
        out[name] = jnp.asarray(drawn.astype(out[name].dtype))
    for name, factor in factors.items():
        out[name] = (out[name] * factor).astype(out[name].dtype)
    return out
```

```python
from contextlib import ExitStack

import numpy as np

import concourse.bass as bass
from concourse import mybir

ALU = mybir.AluOpType
ACT = mybir.ActivationFunctionType
AX = mybir.AxisListType
F32 = mybir.dt.float32
I32 = mybir.dt.int32

P = 128
B, S, D = 4, 1024, 128
TILES = B * S // P
GROUPS = TILES // 4
TB = S // P
NH, HD, ROT = 2, 64, 32
E, HID = 8, 512
HC = HID // P
EPS = 1e-5
BLOCKS = TILES * 2 // 4 + 2
RT = 4 * BLOCKS
NBH = B * NH


def constants():
    f4 = np.float32
    half = np.arange(0, ROT, 2, dtype=f4)
    inv_freq = (f4(1.0) / np.power(f4(10000.0), half / f4(ROT))).astype(f4)
    t = np.arange(S, dtype=f4)
    freqs = np.repeat((t[:, None] * inv_freq).astype(f4), 2, axis=-1).astype(np.float64)
    base = ((half + 0.4 * ROT) / (1.4 * ROT)).astype(np.float64)
    scale = base[None, :] ** ((t.astype(np.float64) - S // 2) / 512.0)[:, None]
    scale = np.concatenate((scale, scale), axis=-1)
    sign = np.where(np.arange(ROT) % 2 == 0, -1.0, 1.0)
    cos, sin = np.cos(freqs), np.sin(freqs) * sign
    both = lambda a: np.stack([a * scale, a / scale], 1)
    tiled = lambda a: a.reshape(TB, P, -1).transpose(1, 0, 2).reshape(P, -1)
    gamma = 1.0 - 2.0 ** (-5.0 - np.arange(NH))
    pos = np.arange(S, dtype=np.float64)[:, None]
    row = np.arange(P)
    full = lambda v: np.broadcast_to(np.asarray(v, np.float64), (P, len(v)))
    return {
        "ident": np.eye(P),
        "before": (row[:, None] < row[None, :]) * 1.0,
        "causal": (row[:, None] <= row[None, :]) * 1.0,
        "ones": np.ones((P, 256)),
        "ropec": tiled(both(cos)),
        "ropes": tiled(both(sin)),
        "decq": tiled(gamma[None, :] ** pos),
        "deck": tiled(gamma[None, :] ** -pos),
        "mhalf": np.full((P, 8), -0.5),
        "eps": np.full((P, 4), EPS),
        "em8": full(np.arange(E) - E),
        "slot": full(np.arange(RT) * P),
    }


def pipeline(eng, outer, inner, stages):
    longest = max(lag for lag, _ in stages)
    filled = (longest + 1) // inner + 1
    def step(o, i):
        for lag, fn in stages:
            oo, ii = o + (i - lag) // inner, (i - lag) % inner
            if not isinstance(oo, int) or 0 <= oo < outer:
                fn(oo, ii)

    for o in range(filled):
        for i in range(inner):
            step(o, i)
    if outer - filled == 1:
        filled, o = outer, outer - 1
        for i in range(inner):
            step(o, i)
    if filled < outer:
        with eng.Fori(filled, outer) as o:
            for i in range(inner):
                step(o, i)
    for i in range(longest):
        step(outer, i)


def wait(eng, sem, n):
    if not isinstance(n, int) or n > 0:
        eng.wait_ge(sem, n)


def build(nc, a, const, cols, out):
    with ExitStack() as ctx:
        def sb(name, shape, dt=F32):
            return ctx.enter_context(nc.sbuf_tensor(name, shape, dt))

        def sem(name):
            return ctx.enter_context(nc.semaphore(name))

        bank = [ctx.enter_context(nc.psum_tensor(f"bank{i}", [P, 512], F32)) for i in range(8)]

        slots_x = nc.dram_tensor("slots_x", (RT * P, D), F32, kind="Internal").ap()
        slots_y = nc.dram_tensor("slots_y", (RT * P, D), F32, kind="Internal").ap()

        cst = sb("cst", [P, const.shape[1]])
        C = {k: cst[:, lo:hi] for k, (lo, hi) in cols.items()}
        ident, ones = C["ident"], C["ones"]
        ropec = C["ropec"].rearrange("p (t s d) -> p t s d", t=TB, s=2)
        ropes = C["ropes"].rearrange("p (t s d) -> p t s d", t=TB, s=2)
        decq = C["decq"].rearrange("p (t h) -> p t h", t=TB)
        deck = C["deck"].rearrange("p (t h) -> p t h", t=TB)
        w_in = sb("w_in", [P, 512])
        wo, w1, w2 = sb("wo", [P, D]), sb("w1", [P, D]), sb("w2", [P, D])
        wr = sb("wr", [P, E])
        wfc_s, wproj_s = sb("wfc_s", [P, HID]), sb("wproj_s", [P, HC, D])
        wfc, wproj = sb("wfc", [P, E * HID]), sb("wproj", [P, E * HC * D])
        bproj = sb("bproj", [E, D])
        rows = sb("rows", [48, P])
        vec = sb("vec", [P, 48])
        out_rows = sb("out_rows", [2, D])
        out_bias = sb("out_bias", [P, D])
        gn_rows = sb("gn_rows", [1, 4])
        gn = sb("gn", [P, 4])
        R_FC, R_FCS, R_L1W, R_L1B, R_L2W, R_L2B, R_W1B = 0, 32, 36, 37, 38, 39, 40
        N_ROWS = 41

        x_all = sb("x_all", [P, TILES, D])
        xn_all = sb("xn_all", [P, TILES, D])
        xnT = sb("xnT", [P, TILES * P])
        hT = sb("hT", [P, TILES * P])
        gate_all = sb("gate_all", [P, TILES, D])
        ret_all = sb("ret_all", [P, TILES, D])

        stats = sb("stats", [P, 2, 4, 6])
        mv = sb("mv", [P, 2, 4, 2])
        ve = sb("ve", [P, 2, 4])
        ra, rb, rc = sb("ra", [P, 2, 4]), sb("rb", [P, 2, 4]), sb("rc", [P, 4])
        xr, hr = sb("xr", [P, 2, 4, D]), sb("hr", [P, 2, 4, D])
        tr = sb("tr", [P, 2, 512])
        work = sb("work", [P, 4096])
        gs = work[:, :].rearrange("p (r c n) -> p r c n", r=2, c=HC)
        xin = work[:, 0:1024].rearrange("p (r u n) -> p r u n", r=2, u=4)
        hs = work[:, 1024:2048].rearrange("p (r n) -> p r n", r=2)
        hb = work[:, 2048:3072].rearrange("p (r n) -> p r n", r=2)
        gt = work[:, 3072:4096].rearrange("p (r n) -> p r n", r=2)
        xts = sb("xts", [P, 2, P])
        ys = sb("ys", [P, 2, 4, D])
        yn_r = ys
        zeros = sb("zeros", [P, 256])
        raw = work[:, 0:1536].rearrange("p (r n) -> p r n", r=4)
        qk = work[:, 1536:2560].rearrange("p (r n) -> p r n", r=4)
        rt1_r, rt2_r = sb("rt1", [P, 2, 2, NH, ROT]), sb("rt2", [P, 2, 2, NH, ROT])
        vd = work[:, 2560:3072].rearrange("p (r n) -> p r n", r=4)
        kT = sb("kT", [P, 4, P])
        qz = sb("qz", [P, 4, NH, P])
        stm = work[:, 3072:4096].rearrange("p (r h n) -> p r h n", r=4, h=NH)
        rs = sb("rs", [P, 4, D])
        yg = sb("yg", [P, 4, 2, D])
        ob = wfc[:, 3072:4096].rearrange("p (r u n) -> p r u n", r=2, u=4)
        lg = sb("lg", [P, TILES, E])
        oh1, oh2 = sb("oh1", [P, TILES, E]), sb("oh2", [P, TILES, E])
        spare = ret_all[:, :, :].rearrange("p t d -> p (t d)")
        ta, tb = (spare[:, j * 256:(j + 1) * 256].rearrange("p (t e) -> p t e", e=E) for j in range(2))
        m1, m2, im = sb("m1", [P, TILES]), sb("m2", [P, TILES]), sb("im", [P, TILES])
        dd, g1, g2 = sb("dd", [P, TILES]), sb("g1", [P, TILES]), sb("g2", [P, TILES])
        gate = sb("gate", [P, TILES, E])
        tot, cum, posn = (spare[:, j * 256:(j + 1) * 256].rearrange("p (e t) -> p e t", e=E) for j in range(2, 5))
        cnt, pad, endp, adj = (sb(n, [P, E]) for n in ("cnt", "pad", "endp", "adj"))
        cnti = sb("cnti", [P, E], I32)
        idx1, idx2 = sb("idx1", [P, TILES], I32), sb("idx2", [P, TILES], I32)
        ended = ret_all[0:1, :, :].rearrange("p t d -> p (t d)")[:, 1280:1280 + RT * E].rearrange("p (j e) -> p j e", e=E)
        tile_e = sb("tile_e", [1, RT])
        off_w, off_b = sb("off_w", [1, RT], I32), sb("off_b", [1, RT], I32)
        gsum, gsq = sb("gsum", [P, NBH]), sb("gsq", [P, NBH])
        squares = wproj[:, :].rearrange("p (j t d) -> p j t d", j=NBH, t=TB)
        gnm, gva, gvb, gac = sb("gnm", [P, NBH]), sb("gva", [P, NBH]), sb("gvb", [P, NBH]), sb("gac", [P, 2, NBH])
        yT, zT, aT = (wfc[:, j * 1024:(j + 1) * 1024].rearrange("p (r n) -> p r n", r=2) for j in range(3))
        gr = sb("gr", [P, 2, 4, E])
        gT = sb("gT", [E, 2, 512])

        names = """cst_in vec_in win_in wr_in wshared_in wexp_in watt_in zero_in x_in0 x_in1 xn_kept0 xn_kept1
            zeroed pre_pe pre_act ve_ready r_ready xn_done tr_ready xnt_done ht_done lg_ready link_v link_p
            mask_ready rank_ready dd_ready ex_ready gates_ready idx_ready off_ready scattered
            fc_ready gs_done proj_ready acc_done
            xs_in0 xs_in1 xt_ready xt_copied h_ready hs_copied ht2_ready hb_done gelu_done y_ready ys_done st_done0 st_done1
            hr_in0 hr_in1 qkvg_ready raw_ready gate_kept roped vd_done qkt_ready kt_copied st_ready masked state_ready r_copied
            o_ready ret_done gath0 gath1 gath2 gath3 combined qz_zero
            gsum_ready gtot_ready gmean_ready gsq_ready gtot2_ready gve_ready gr_ready gac_ready mish_in mish_exp mish_done
            rsq sp_passed stats_landed st1 ag1 st2 ag2 bias_done rot_parts part_sums xy_done yn_done yr_done gr_done tg_ready t1_ready yt_copied gt8_copied wo_ready y2_done ve2_ready r2_ready z0_done t2_ready zt_done
            m1_ready at_done m2_ready fin_ready out_done0 out_done1""".split()
        s = {n: sem(n) for n in names}
        block = ctx.enter_context(nc.Block())

        x_d = a["L0_attn_x"].rearrange("b (t p) d -> p (b t) d", p=P)
        out_d = out.rearrange("b (t p) d -> p (b t) d", p=P)
        one_row = lambda v: v.rearrange("(o n) -> o n", o=1)

        @block.sync
        def _(sp):
            def sp_wait(sem, n):
                wait(sp, sem, n)
                if not isinstance(n, int):
                    sp.sem_inc(s["sp_passed"], 1)

            sp.dma_start(cst[:, :], const).then_inc(s["cst_in"], 16)

            def load_x(o, i):
                n, t = 16 * o, 8 * o + 4 * i
                sp_wait(s[f"x_in{i}"], n)
                sp.dma_start(x_all[:, bass.ds(t, 4), :], x_d[:, bass.ds(t, 4), :]).then_inc(s[f"x_in{i}"], 16)

            def keep_xn(o, i):
                done, n, t = 2 * o + i + 1, 16 * o, 8 * o + 4 * i
                sp_wait(s["xn_done"], done)
                sp_wait(s[f"xn_kept{i}"], n)
                sp.dma_start(xn_all[:, bass.ds(t, 4), :], xr[:, i, :, :]).then_inc(s[f"xn_kept{i}"], 16)

            load_x(0, 0)
            for i, v in enumerate((a["L0_attn_ln1_w"], a["L0_attn_ln1_b"], a["L0_attn_ln2_w"], a["L0_attn_ln2_b"], a["L0_attn_w1_b"])):
                sp.dma_start(rows[R_L1W + i:R_L1W + i + 1, :], one_row(v)).then_inc(s["vec_in"], 16)
            sp.dma_start(rows[R_FC:R_FC + E * HC, :], a["L0_ffn_bfc"].rearrange("e (c p) -> (e c) p", p=P)).then_inc(s["vec_in"], 16)
            sp.dma_start(rows[R_FCS:R_FCS + HC, :], a["L0_ffn_bfc_s"].rearrange("(c p) -> c p", p=P)).then_inc(s["vec_in"], 16)
            sp.dma_start(out_rows[0:1, :], one_row(a["L0_attn_w2_b"])).then_inc(s["vec_in"], 16)
            sp.dma_start(out_rows[1:2, :], one_row(a["L0_ffn_bproj_s"])).then_inc(s["vec_in"], 16)
            sp.dma_start(gn_rows[0:1, 0:2], one_row(a["L0_attn_gn_w"])).then_inc(s["vec_in"], 16)
            sp.dma_start(gn_rows[0:1, 2:4], one_row(a["L0_attn_gn_b"])).then_inc(s["vec_in"], 16)
            load_x(0, 1)
            sp.dma_start(wr[:, :], a["L0_ffn_Wr"]).then_inc(s["wr_in"], 16)
            pipeline(sp, 4, 2, [(0, lambda o, i: load_x(o, i) if not isinstance(o, int) or o else None), (2, keep_xn)])
            sp.dma_start(wfc_s[:, :], a["L0_ffn_Wfc_s"]).then_inc(s["wshared_in"], 16)
            sp.dma_start(wproj_s[:, :, :], a["L0_ffn_Wproj_s"].rearrange("(c p) d -> p c d", p=P)).then_inc(s["wshared_in"], 16)
            sp.wait_ge(s["zero_in"], 1)
            sp.dma_start(slots_x.rearrange("(p q n) d -> p q (n d)", p=P, n=2), zeros[:, :].unsqueeze(1).broadcast_to([P, RT // 2, 256])).then_inc(s["zeroed"], 16)
            sp.dma_start(wfc[:, :].rearrange("p (e n) -> p e n", e=E), a["L0_ffn_Wfc"].rearrange("e p n -> p e n")).then_inc(s["wexp_in"], 16)
            sp.dma_start(wproj[:, :].rearrange("p (e c d) -> p e c d", e=E, c=HC), a["L0_ffn_Wproj"].rearrange("e (c p) d -> p e c d", p=P)).then_inc(s["wexp_in"], 16)
            for h in range(NH):
                sp.dma_start(w_in[:, 0:384].rearrange("p (s h d) -> p s h d", s=3, h=NH)[:, :, h, :],
                             a["L0_attn_wqkv_w"].rearrange("p (h s d) -> p s h d", h=NH, s=3)[:, :, h, :]).then_inc(s["win_in"], 16)
            sp.dma_start(w_in[:, 384:512], a["L0_attn_wg_w"]).then_inc(s["win_in"], 16)
            for w, v in ((wo, "wo"), (w1, "w1"), (w2, "w2")):
                sp.dma_start(w[:, :], a[f"L0_attn_{v}_w"]).then_inc(s["watt_in"], 16)
            sp.dma_start(bproj[:, :], a["L0_ffn_bproj"]).then_inc(s["watt_in"], 16)

            def load_slots(o, i):
                read, n, q = 8 * o + 4 * i - 4, 16 * o, 2 * o + i
                sp_wait(s["xt_ready"], read)
                sp_wait(s[f"xs_in{i}"], n)
                sp.dma_start(xin[:, i, :, :], slots_x.rearrange("(q u p) d -> q p u d", u=4, p=P)[bass.ds(q, 1)].rearrange("q p u d -> p (q u) d")).then_inc(s[f"xs_in{i}"], 16)

            def store_slots(o, i):
                done, n, q = 8 * o + 4 * i + 4, 16 * o, 2 * o + i
                sp_wait(s["ys_done"], done)
                sp_wait(s[f"st_done{i}"], n)
                sp.dma_start(slots_y.rearrange("(q u p) d -> q p u d", u=4, p=P)[bass.ds(q, 1)].rearrange("q p u d -> p (q u) d"), ys[:, i, :, :]).then_inc(s[f"st_done{i}"], 16)

            sp.wait_ge(s["scattered"], 16 * 2 * TILES)
            sp.wait_ge(s["proj_ready"], GROUPS)
            pipeline(sp, BLOCKS // 2, 2, [(0, load_slots), (2, store_slots)])

            def load_hr(o, i):
                read, n, t = 8 * o + 4 * i - 4, 16 * o, (2 * o + i) * 512
                sp_wait(s["qkvg_ready"], read)
                sp_wait(s[f"hr_in{i}"], n)
                sp.dma_start(tr[:, i, :], hT[:, bass.ds(t, 512)]).then_inc(s[f"hr_in{i}"], 16)

            pipeline(sp, B, 2, [(0, load_hr)])

            def store_out(o, i):
                done, n, t = 2 * o + i + 1, 16 * o, 8 * o + 4 * i
                sp_wait(s["fin_ready"], done)
                sp_wait(s[f"out_done{i}"], n)
                sp.dma_start(out_d[:, bass.ds(t, 4), :], ob[:, i, :, :]).then_inc(s[f"out_done{i}"], 16)

            pipeline(sp, B, 2, [(0, store_out)])
            sp.wait_ge(s["out_done0"], 16 * B)
            sp.wait_ge(s["out_done1"], 16 * B)

        @block.tensor
        def _(pe):
            pe.wait_ge(s["cst_in"], 16)
            pe.wait_ge(s["vec_in"], 16 * 11)
            pe.transpose(bank[5][:, 0:N_ROWS], rows[0:N_ROWS, :], ident[0:N_ROWS, 0:N_ROWS])
            pe.matmul(bank[6][:, 0:D], ones[0:2, 0:P], out_rows[:, :], start=True, stop=True)
            pe.matmul(bank[6][:, D:D + 4], ones[0:1, 0:P], gn_rows[:, :], start=True, stop=True).then_inc(s["pre_pe"], 1)
            pe.wait_ge(s["wr_in"], 16)

            def p1_transpose(o, i):
                k = 2 * o + i
                pe.wait_ge(s["xn_done"], k + 1)
                wait(pe, s["ht_done"], k - 1)
                for u in range(4):
                    pe.transpose(bank[i][:, u * P:(u + 1) * P], xr[:, i, u, :], ident)
                for u in range(4):
                    last = pe.transpose(bank[2 + i][:, u * P:(u + 1) * P], hr[:, i, u, :], ident)
                last.then_inc(s["tr_ready"], 1)

            def p1_logits(o, i):
                k = 2 * o + i
                pe.wait_ge(s["xnt_done"], k + 1)
                for u in range(4):
                    last = pe.matmul(bank[4][:, bass.ds(k * 4 * E + u * E, E)], tr[:, i, u * P:(u + 1) * P], wr[:, :], start=True, stop=True)
                last.then_inc(s["lg_ready"], 1)

            pipeline(pe, 4, 2, [(0, p1_transpose), (1, p1_logits)])

            def ranks():
                pe.wait_ge(s["mask_ready"], 1)
                pe.matmul(bank[5][:, 0:256], C["before"], ta[:, :, :].rearrange("p t e -> p (t e)"), start=True, stop=True)
                pe.matmul(bank[6][:, 0:256], ones[:, 0:P], ta[:, :, :].rearrange("p t e -> p (t e)"), start=True, stop=True).then_inc(s["rank_ready"], 1)

            def fc(o, i):
                k = 2 * o + i
                for c in range(HC):
                    wait(pe, s["gs_done"], HC * (k - 1) + c + 1)
                    pe.matmul(bank[c][:, :], wfc_s[:, c * P:(c + 1) * P], xnT[:, bass.ds(k * 512, 512)], start=True, stop=True).then_inc(s["fc_ready"], 1)

            def proj(o, i):
                k = 2 * o + i
                pe.wait_ge(s["gs_done"], HC * (k + 1))
                wait(pe, s["acc_done"], k)
                for u in range(4):
                    for c in range(HC):
                        last = pe.matmul(bank[7][:, u * P:(u + 1) * P], gs[:, i, c, u * P:(u + 1) * P], wproj_s[:, c, :], start=(c == 0), stop=(c == HC - 1))
                last.then_inc(s["proj_ready"], 1)

            pe.wait_ge(s["wshared_in"], 32)
            pe.wait_ge(s["ht_done"], GROUPS)
            ranks()
            pipeline(pe, 4, 2, [(0, fc), (1, proj)])

            pe.wait_ge(s["off_ready"], 1)
            pe.wait_ge(s["wexp_in"], 32)
            pe.wait_ge(s["acc_done"], GROUPS)

            def expert(o, i):
                return pe.value_load(off_w[0:1, bass.ds(8 * o + i, 1)], min_val=0, max_val=(E - 1) * HID)

            def x_transpose(o, i):
                k = 8 * o + i
                if i % 4 == 0:
                    pe.wait_ge(s[f"xs_in{i // 4}"], 16 * (o + 1))
                wait(pe, s["xt_copied"], k)
                pe.transpose(bank[0][:, 0:P], xin[:, i // 4, i % 4, :], ident).then_inc(s["xt_ready"], 1)

            def up(o, i):
                k = 8 * o + i
                e = expert(o, i)
                pe.wait_ge(s["xt_copied"], k + 1)
                wait(pe, s["hs_copied"], k - 1)
                pe.matmul(bank[1 + i % 2][:, :], xts[:, i % 2, :], wfc[:, bass.ds(e, HID)], start=True, stop=True).then_inc(s["h_ready"], 1)

            def h_transpose(o, i):
                k = 8 * o + i
                pe.wait_ge(s["hs_copied"], k + 1)
                wait(pe, s["hb_done"], k - 1)
                for c in range(HC):
                    last = pe.transpose(bank[3 + i % 2][:, c * P:(c + 1) * P], hs[:, i % 2, c * P:(c + 1) * P], ident)
                last.then_inc(s["ht2_ready"], 1)

            def down(o, i):
                k = 8 * o + i
                e = expert(o, i)
                pe.wait_ge(s["gelu_done"], k + 1)
                wait(pe, s["ys_done"], k - 1)
                for c in range(HC):
                    last = pe.matmul(bank[5 + i % 2][:, 0:D], gt[:, i % 2, c * P:(c + 1) * P], wproj[:, bass.ds(e + c * D, D)], start=(c == 0), stop=(c == HC - 1))
                last.then_inc(s["y_ready"], 1)

            pipeline(pe, RT // 8, 8, [(0, x_transpose), (1, up), (4, down), (2, h_transpose)])

            pe.wait_ge(s["win_in"], 48)
            pe.wait_ge(s["ys_done"], RT)
            pe.wait_ge(s["qz_zero"], 1)

            def project(b, u):
                k = TB * b + u
                if u % 4 == 0:
                    pe.wait_ge(s[f"hr_in{u // 4}"], 16 * (b + 1))
                wait(pe, s["gate_kept"], k - 1)
                pe.matmul(bank[u % 2][:, :], tr[:, u // 4, (u % 4) * P:(u % 4 + 1) * P], w_in[:, :], start=True, stop=True).then_inc(s["qkvg_ready"], 1)

            def qk_transpose(b, u):
                k = TB * b + u
                pe.wait_ge(s["roped"], k + 1)
                wait(pe, s["kt_copied"], k - 1)
                for j in range(2):
                    last = pe.transpose(bank[2 + u % 2][:, j * P:(j + 1) * P], qk[:, u % 4, j * P:(j + 1) * P], ident)
                last.then_inc(s["qkt_ready"], 1)

            def scores(b, u):
                k = TB * b + u
                pe.wait_ge(s["kt_copied"], k + 1)
                wait(pe, s["masked"], k)
                pe.matmul(bank[4][:, 0:NH * P], kT[:, u % 4, :], qz[:, u % 4, :, :].rearrange("p h n -> p (h n)"), start=True, stop=True).then_inc(s["st_ready"], 1)
                pe.wait_ge(s["vd_done"], k + 1)
                wait(pe, s["r_copied"], k)
                pe.matmul(bank[5][:, 0:D], qk[:, u % 4, P:2 * P], vd[:, u % 4, :], start=(u == 0), stop=True, skip_group_check=True).then_inc(s["state_ready"], 1)

            def outputs(b, u):
                k = TB * b + u
                pe.wait_ge(s["masked"], k + 1)
                wait(pe, s["r_copied"], k)
                wait(pe, s["ret_done"], k - 1)
                for h in range(NH):
                    o_h = bank[6 + u % 2][:, h * HD:(h + 1) * HD]
                    last = pe.matmul(o_h, stm[:, u % 4, h, :], vd[:, u % 4, h * HD:(h + 1) * HD], start=True, stop=(u == 0))
                    if u > 0:
                        last = pe.matmul(o_h, qz[:, u % 4, h, :], rs[:, (u - 1) % 4, h * HD:(h + 1) * HD], start=False, stop=True)
                last.then_inc(s["o_ready"], 1)

            pipeline(pe, B, TB, [(0, project), (2, qk_transpose), (4, outputs), (3, scores)])

            for step in ("gsum", "gsq"):
                pe.wait_ge(s[f"{step}_ready"], B if step == "gsum" else NBH)
                pe.matmul(bank[0][:, 0:NBH], ones[:, 0:P], (gsum if step == "gsum" else gsq)[:, :], start=True, stop=True).then_inc(s["gtot_ready" if step == "gsum" else "gtot2_ready"], 1)

            pe.wait_ge(s["watt_in"], 64)
            pe.wait_ge(s["ret_done"], TILES)
            pe.wait_ge(s["gac_ready"], 1)

            def y_transpose(o, i):
                k = 2 * o + i
                pe.wait_ge(s["yr_done"], k + 1)
                wait(pe, s["yt_copied"], k)
                for u in range(4):
                    last = pe.transpose(bank[0][:, u * P:(u + 1) * P], hr[:, i, u, :], ident)
                last.then_inc(s["t1_ready"], 1)

            def gate_transpose(o, i):
                k = 2 * o + i
                pe.wait_ge(s["gr_done"], k + 1)
                wait(pe, s["gt8_copied"], k)
                for u in range(4):
                    last = pe.transpose(bank[1][0:E, u * P:(u + 1) * P], gr[:, i, u, :], ident)
                last.then_inc(s["tg_ready"], 1)

            def wo_mm(o, i):
                k = 2 * o + i
                pe.wait_ge(s["yt_copied"], k + 1)
                wait(pe, s["y2_done"], k)
                for u in range(4):
                    last = pe.matmul(bank[2][:, u * P:(u + 1) * P], yT[:, i, u * P:(u + 1) * P], wo[:, :], start=True, stop=True)
                last.then_inc(s["wo_ready"], 1)

            def z_transpose(o, i):
                k = 2 * o + i
                pe.wait_ge(s["z0_done"], k + 1)
                wait(pe, s["zt_done"], k)
                for u in range(4):
                    last = pe.transpose(bank[3][:, u * P:(u + 1) * P], xr[:, i, u, :], ident)
                last.then_inc(s["t2_ready"], 1)

            def w1_mm(o, i):
                k = 2 * o + i
                pe.wait_ge(s["zt_done"], k + 1)
                wait(pe, s["at_done"], k)
                pe.matmul(bank[4][:, :], w1[:, :], zT[:, i, :], start=True, stop=True).then_inc(s["m1_ready"], 1)

            def w2_mm(o, i):
                k = 2 * o + i
                pe.wait_ge(s["at_done"], k + 1)
                pe.wait_ge(s["gt8_copied"], k + 1)
                wait(pe, s["fin_ready"], k)
                for u in range(4):
                    pe.matmul(bank[5][:, u * P:(u + 1) * P], aT[:, i, u * P:(u + 1) * P], w2[:, :], start=True, stop=False)
                    last = pe.matmul(bank[5][:, u * P:(u + 1) * P], gT[:, i, u * P:(u + 1) * P], bproj[:, :], start=False, stop=True)
                last.then_inc(s["m2_ready"], 1)

            pipeline(pe, B, 2, [(0, y_transpose), (1, wo_mm), (4, w1_mm), (4, gate_transpose), (5, w2_mm), (3, z_transpose)])

        @block.scalar
        def _(act):
            act.wait_ge(s["pre_pe"], 1)
            act.activation(vec[:, 0:N_ROWS], bank[5][:, 0:N_ROWS], ACT.Copy)
            act.activation(out_bias[:, :], bank[6][:, 0:D], ACT.Copy)
            act.activation(gn[:, :], bank[6][:, D:D + 4], ACT.Copy).then_inc(s["pre_act"], 1)
            act.wait_ge(s["pre_act"], 1)

            def p1_copy(o, i):
                k = 2 * o + i
                act.wait_ge(s["tr_ready"], k + 1)
                wait(act, s["lg_ready"], k - 1)
                act.activation(tr[:, i, :], bank[i][:, :], ACT.Copy).then_inc(s["xnt_done"], 1)
                act.activation(xnT[:, bass.ds(k * 512, 512)], bank[i][:, :], ACT.Copy)
                act.activation(hT[:, bass.ds(k * 512, 512)], bank[2 + i][:, :], ACT.Identity, bias=vec[:, R_L1B:R_L1B + 1], scale=vec[:, R_L1W:R_L1W + 1]).then_inc(s["ht_done"], 1)

            pipeline(act, 4, 2, [(0, p1_copy)])
            act.wait_ge(s["dd_ready"], 1)
            act.activation(g2[:, :], dd[:, :], ACT.Exp).then_inc(s["ex_ready"], 1)

            def shared_gelu(o, i):
                k = 2 * o + i
                wait(act, s["proj_ready"], k - 1)
                for c in range(HC):
                    act.wait_ge(s["fc_ready"], HC * k + c + 1)
                    act.activation(gs[:, i, c, :], bank[c][:, :], ACT.Gelu_apprx_tanh, bias=vec[:, R_FCS + c:R_FCS + c + 1]).then_inc(s["gs_done"], 1)

            pipeline(act, 4, 2, [(0, shared_gelu)])
            act.wait_ge(s["proj_ready"], GROUPS)

            def xt_copy(o, i):
                k = 8 * o + i
                act.wait_ge(s["xt_ready"], k + 1)
                wait(act, s["h_ready"], k - 1)
                act.activation(xts[:, i % 2, :], bank[0][:, 0:P], ACT.Copy).then_inc(s["xt_copied"], 1)

            def h_copy(o, i):
                k = 8 * o + i
                act.wait_ge(s["h_ready"], k + 1)
                wait(act, s["ht2_ready"], k - 1)
                act.activation(hs[:, i % 2, :], bank[1 + i % 2][:, :], ACT.Copy).then_inc(s["hs_copied"], 1)

            def gelu(o, i):
                k = 8 * o + i
                act.wait_ge(s["hb_done"], k + 1)
                wait(act, s["y_ready"], k - 1)
                act.activation(gt[:, i % 2, :], hb[:, i % 2, :], ACT.Gelu_apprx_tanh).then_inc(s["gelu_done"], 1)

            pipeline(act, RT // 8, 8, [(0, xt_copy), (1, h_copy), (2, gelu)])

            act.wait_ge(s["qz_zero"], 1)

            def qkv_copy(b, u):
                k = TB * b + u
                act.wait_ge(s["qkvg_ready"], k + 1)
                wait(act, s["roped"], k - 3)
                wait(act, s["vd_done"], k - 3)
                act.activation(raw[:, u % 4, :], bank[u % 2][:, 0:384], ACT.Copy).then_inc(s["raw_ready"], 1)
                act.activation(gate_all[:, bass.ds(k, 1), :].rearrange("p t d -> p (t d)"), bank[u % 2][:, 384:512], ACT.Copy).then_inc(s["gate_kept"], 1)

            def kt_copy(b, u):
                k = TB * b + u
                act.wait_ge(s["qkt_ready"], k + 1)
                wait(act, s["o_ready"], k - 3)
                for h in range(NH):
                    act.activation(qz[h * HD:(h + 1) * HD, u % 4, h, :], bank[2 + u % 2][h * HD:(h + 1) * HD, 0:P], ACT.Copy)
                act.activation(kT[:, u % 4, :], bank[2 + u % 2][:, P:2 * P], ACT.Copy).then_inc(s["kt_copied"], 1)

            def r_copy(b, u):
                k = TB * b + u
                act.wait_ge(s["state_ready"], k + 1)
                wait(act, s["o_ready"], k - 2)
                act.activation(rs[:, u % 4, :], bank[5][:, 0:D], ACT.Copy).then_inc(s["r_copied"], 1)

            pipeline(act, B, TB, [(0, qkv_copy), (2, kt_copy), (3, r_copy)])

            act.wait_ge(s["gmean_ready"], 1)
            for b in range(B):
                for h in range(NH):
                    j = NH * b + h
                    act.activation(squares[:, j, :, :], ret_all[:, TB * b:TB * (b + 1), h * HD:(h + 1) * HD], ACT.Square, bias=gnm[:, j:j + 1], accum_out=gsq[:, j:j + 1]).then_inc(s["gsq_ready"], 1)
            for b in range(B):
                act.wait_ge(s["mish_in"], b + 1)
                act.activation(xnT[:, b * 1024:(b + 1) * 1024], xnT[:, b * 1024:(b + 1) * 1024], ACT.Exp).then_inc(s["mish_exp"], 1)
            act.wait_ge(s["gac_ready"], 1)
            for i in range(2):
                act.wait_ge(s[f"st_done{i}"], 16 * BLOCKS // 2)

            def yn(o, i):
                k = 2 * o + i
                wait(act, s["yr_done"], k - 1)
                for h in range(NH):
                    last = act.activation(yn_r[:, i, :, h * HD:(h + 1) * HD], ret_all[:, bass.ds(4 * k, 4), h * HD:(h + 1) * HD], ACT.Identity,
                                          bias=gac[:, 1, bass.ds(NH * o + h, 1)], scale=gac[:, 0, bass.ds(NH * o + h, 1)])
                last.then_inc(s["yn_done"], 1)

            def y_copy(o, i):
                k = 2 * o + i
                act.wait_ge(s["t1_ready"], k + 1)
                wait(act, s["wo_ready"], k - 1)
                act.activation(yT[:, i, :], bank[0][:, :], ACT.Copy).then_inc(s["yt_copied"], 1)

            def z_copy(o, i):
                k = 2 * o + i
                act.wait_ge(s["t2_ready"], k + 1)
                wait(act, s["m1_ready"], k - 1)
                act.activation(zT[:, i, :], bank[3][:, :], ACT.Identity, bias=vec[:, R_L2B:R_L2B + 1], scale=vec[:, R_L2W:R_L2W + 1]).then_inc(s["zt_done"], 1)

            def ffn_gelu(o, i):
                k = 2 * o + i
                act.wait_ge(s["m1_ready"], k + 1)
                wait(act, s["m2_ready"], k - 1)
                act.activation(aT[:, i, :], bank[4][:, :], ACT.Gelu, bias=vec[:, R_W1B:R_W1B + 1]).then_inc(s["at_done"], 1)
                act.wait_ge(s["tg_ready"], k + 1)
                act.activation(gT[:, i, :], bank[1][0:E, :], ACT.Copy).then_inc(s["gt8_copied"], 1)

            pipeline(act, B, 2, [(0, yn), (0, y_copy), (3, z_copy), (4, ffn_gelu)])

        @block.gpsimd
        def _(pool):
            pool.memset(zeros[:, :], 0.0).then_inc(s["zero_in"], 1)
            pool.memset(qz[:, :, :, :], 0.0).then_inc(s["qz_zero"], 1)
            pool.wait_ge(s["cst_in"], 16)
            chain = [0]

            def link(ins):
                chain[0] += 1
                ins.then_inc(s["link_p"], 1)
                pool.wait_ge(s["link_p"], chain[0])

            def rsqrt(o, i):
                k = 2 * o + i
                n = 5 * k
                pool.wait_ge(s["ve_ready"], k + 1)
                wait(pool, s["xn_done"], k - 1)
                v = mv[:, i, :, 1]
                steps = (
                    lambda: pool.tensor_tensor(ra[:, i, :], ve[:, i, :], C["mhalf"][:, 0:4], ALU.pow),
                    lambda: pool.tensor_tensor(rb[:, i, :], v, ra[:, i, :], ALU.mult),
                    lambda: pool.tensor_tensor(rb[:, i, :], rb[:, i, :], ra[:, i, :], ALU.mult),
                    lambda: pool.tensor_tensor(rc[:, :], rb[:, i, :], C["eps"], ALU.add),
                    lambda: pool.tensor_tensor(rb[:, i, :], rc[:, :], C["mhalf"][:, 0:4], ALU.pow),
                )
                for j, f in enumerate(steps):
                    f().then_inc(s["rsq"], 1)
                    pool.wait_ge(s["rsq"], n + j + 1)
                pool.tensor_tensor(rb[:, i, :], rb[:, i, :], ra[:, i, :], ALU.mult).then_inc(s["r_ready"], 1)

            pipeline(pool, 4, 2, [(0, rsqrt)])

            pool.wait_ge(s["idx_ready"], 1)
            for i in range(2):
                pool.wait_ge(s[f"xn_kept{i}"], 16 * 4)
            pool.wait_ge(s["zeroed"], 16)
            for t in range(TILES):
                for idx in (idx1, idx2):
                    pool.indirect_dma_start(out=slots_x, out_offset=bass.IndirectOffsetOnAxis(ap=idx[:, t:t + 1], axis=0),
                                            in_=xn_all[:, t, :], in_offset=None).then_inc(s["scattered"], 16)

            for i in range(2):
                pool.wait_ge(s[f"st_done{i}"], 16 * BLOCKS // 2)
            for t in range(TILES):
                u = t % TB
                if t >= 4:
                    pool.wait_ge(s["combined"], t - 3)
                for j, idx in enumerate((idx1, idx2)):
                    pool.indirect_dma_start(out=yg[:, t % 4, j, :], out_offset=None, in_=slots_y,
                                            in_offset=bass.IndirectOffsetOnAxis(ap=idx[:, t:t + 1], axis=0)).then_inc(s[f"gath{t % 4}"], 16)
                pool.wait_ge(s["raw_ready"], t + 1)
                if t >= 4:
                    pool.wait_ge(s["o_ready"], t - 3)
                pool.tensor_tensor(vd[:, t % 4, :].rearrange("p (h d) -> p h d", h=NH), raw[:, t % 4, 256:384].rearrange("p (h d) -> p h d", h=NH),
                                   deck[:, u, :].unsqueeze(2).broadcast_to([P, NH, HD]), ALU.mult).then_inc(s["vd_done"], 1)

            pool.wait_ge(s["gve_ready"], 1)
            pool.tensor_tensor(gvb[:, :], gva[:, :], C["mhalf"], ALU.pow).then_inc(s["gr_ready"], 1)

            def rsqrt2(o, i):
                k = 2 * o + i
                pool.wait_ge(s["ve2_ready"], k + 1)
                wait(pool, s["z0_done"], k - 1)
                pool.tensor_tensor(ra[:, i, :], ve[:, i, :], C["mhalf"][:, 0:4], ALU.pow).then_inc(s["r2_ready"], 1)

            pipeline(pool, B, 2, [(0, rsqrt2)])

        @block.vector
        def _(dve):
            chain = [0]

            def link(ins):
                chain[0] += 1
                ins.then_inc(s["link_v"], 1)
                dve.wait_ge(s["link_v"], chain[0])

            def moments(x4, i, k, stat, aggr, ready):
                for u in range(4):
                    last = dve.bn_stats(stats[:, i, u, :], x4(u))
                last.then_inc(s[stat], 1)
                dve.wait_ge(s[stat], k + 1)
                dve.sem_inc(s["stats_landed"], 1)
                for u in range(4):
                    last = dve.bn_aggr(mv[:, i, u, :], stats[:, i, u, :])
                last.then_inc(s[aggr], 1)
                dve.wait_ge(s[aggr], k + 1)
                dve.tensor_scalar(ve[:, i, :], mv[:, i, :, 1], EPS, None, ALU.add).then_inc(s[ready], 1)

            def p1_moments(o, i):
                k = 2 * o + i
                dve.wait_ge(s[f"x_in{i}"], 16 * (o + 1))
                moments(lambda u: x_all[:, bass.ds(4 * k + u, 1), :].rearrange("p t d -> p (t d)"), i, k, "st1", "ag1", "ve_ready")

            def p1_norm(o, i):
                k = 2 * o + i
                dve.wait_ge(s["r_ready"], k + 1)
                wait(dve, s[f"xn_kept{i}"], 16 * o)
                wait(dve, s["tr_ready"], k - 1)
                for r, ring in ((ra, xr), (rb, hr)):
                    for u in range(4):
                        last = dve.tensor_scalar(ring[:, i, u, :], x_all[:, bass.ds(4 * k + u, 1), :].rearrange("p t d -> p (t d)"),
                                                 mv[:, i, u, 0:1], r[:, i, u:u + 1], ALU.subtract, ALU.mult)
                last.then_inc(s["xn_done"], 1)

            pipeline(dve, 4, 2, [(0, p1_moments), (1, p1_norm)])

            em8 = C["em8"].unsqueeze(1).broadcast_to([P, TILES, E])
            wide = lambda m: m[:, :].unsqueeze(2).broadcast_to([P, TILES, E])
            by_e = lambda m: m.rearrange("p t e -> p e t")
            dve.wait_ge(s["lg_ready"], GROUPS)
            link(dve.tensor_copy(lg[:, :, :].rearrange("p t e -> p (t e)"), bank[4][:, 0:256]))
            for m, oh in ((m1, oh1), (m2, oh2)):
                src = lg if m is m1 else tb
                link(dve.tensor_reduce(m[:, :], src[:, :, :], AX.X, ALU.max))
                link(dve.tensor_tensor(ta[:, :, :], src[:, :, :], wide(m), ALU.is_equal))
                link(dve.tensor_tensor(ta[:, :, :], ta[:, :, :], em8, ALU.mult))
                link(dve.tensor_reduce(im[:, :], ta[:, :, :], AX.X, ALU.min))
                link(dve.tensor_tensor(oh[:, :, :], em8, wide(im), ALU.is_equal))
                if m is m1:
                    link(dve.scalar_tensor_tensor(tb[:, :, :], oh[:, :, :], -3e38, lg[:, :, :], ALU.mult, ALU.add))
            dve.tensor_tensor(ta[:, :, :], oh1[:, :, :], oh2[:, :, :], ALU.add).then_inc(s["mask_ready"], 1)
            dve.tensor_tensor(dd[:, :], m2[:, :], m1[:, :], ALU.subtract).then_inc(s["dd_ready"], 1)
            dve.wait_ge(s["rank_ready"], 1)
            link(dve.tensor_copy(tot[:, :, :], by_e(bank[6][:, 0:256].rearrange("p (t e) -> p t e", e=E))))
            flat = lambda m: m[:, :, :].rearrange("p e t -> p (e t)")
            link(dve.tensor_tensor_scan(flat(cum), C["ones"], flat(tot), 0.0, ALU.mult, ALU.add))
            link(dve.tensor_copy(cnt[:, :], cum[:, :, TILES - 1]))
            link(dve.tensor_tensor(pad[:, 1:E], cnt[:, 1:E], cnt[:, 0:E - 1], ALU.subtract))
            link(dve.tensor_copy(pad[:, 0:1], cnt[:, 0:1]))
            link(dve.tensor_scalar(cnti[:, :], pad[:, :], float(P - 1), None, ALU.add))
            link(dve.tensor_scalar(cnti[:, :], cnti[:, :], 7, 7, ALU.logical_shift_right, ALU.logical_shift_left))
            link(dve.tensor_tensor(adj[:, :], cnt[:, :], pad[:, :], ALU.subtract))
            link(dve.tensor_copy(pad[:, :], cnti[:, :]))
            link(dve.tensor_tensor_scan(endp[:, :], C["ones"][:, 0:E], pad[:, :], 0.0, ALU.mult, ALU.add))
            link(dve.tensor_tensor(pad[:, :], endp[:, :], pad[:, :], ALU.subtract))
            link(dve.tensor_tensor(adj[:, :], pad[:, :], adj[:, :], ALU.subtract))
            link(dve.tensor_tensor(posn[:, :, :], cum[:, :, :], tot[:, :, :], ALU.subtract))
            link(dve.tensor_tensor(posn[:, :, :], posn[:, :, :], adj[:, :].unsqueeze(2).broadcast_to([P, E, TILES]), ALU.add))
            link(dve.tensor_tensor(posn[:, :, :], posn[:, :, :], by_e(bank[5][:, 0:256].rearrange("p (t e) -> p t e", e=E)), ALU.add))
            for oh, idx in ((oh1, idx1), (oh2, idx2)):
                link(dve.tensor_tensor(tb[:, :, :], oh[:, :, :], posn[:, :, :].rearrange("p e t -> p t e"), ALU.mult))
                link(dve.tensor_reduce(im[:, :], tb[:, :, :], AX.X, ALU.add))
                last = dve.tensor_copy(idx[:, :], im[:, :])
                if idx is idx1:
                    link(last)
            last.then_inc(s["idx_ready"], 1)
            link(dve.tensor_tensor(ended[:, :, :], C["slot"][0:1, :].unsqueeze(2).broadcast_to([1, RT, E]), endp[0:1, :].unsqueeze(1).broadcast_to([1, RT, E]), ALU.is_ge))
            link(dve.tensor_reduce(tile_e[:, :], ended[:, :, :], AX.X, ALU.add))
            link(dve.tensor_scalar(tile_e[:, :], tile_e[:, :], float(E - 1), None, ALU.min))
            link(dve.tensor_scalar(off_b[:, :], tile_e[:, :], float(HC), None, ALU.mult))
            dve.tensor_scalar(off_w[:, :], tile_e[:, :], float(HID), None, ALU.mult).then_inc(s["off_ready"], 1)
            dve.wait_ge(s["ex_ready"], 1)
            link(dve.tensor_scalar(g1[:, :], g2[:, :], 1.0, None, ALU.add))
            link(dve.reciprocal(g1[:, :], g1[:, :]))
            link(dve.tensor_tensor(g2[:, :], g2[:, :], g1[:, :], ALU.mult))
            link(dve.tensor_tensor(gate[:, :, :], oh1[:, :, :], wide(g1), ALU.mult))
            link(dve.tensor_tensor(tb[:, :, :], oh2[:, :, :], wide(g2), ALU.mult))
            link(dve.tensor_tensor(gate[:, :, :], gate[:, :, :], tb[:, :, :], ALU.add))

            def acc(o, i):
                k = 2 * o + i
                x4 = x_all[:, bass.ds(4 * k, 4), :]
                dve.wait_ge(s["proj_ready"], k + 1)
                dve.tensor_tensor(x4, x4, bank[7][:, :].rearrange("p (t d) -> p t d", t=4), ALU.add).then_inc(s["acc_done"], 1)
                dve.wait_ge(s["acc_done"], k + 1)
                dve.tensor_tensor(x4, x4, out_bias[:, :].unsqueeze(1).broadcast_to([P, 4, D]), ALU.add).then_inc(s["bias_done"], 1)

            dve.wait_ge(s["pre_act"], 1)
            pipeline(dve, 4, 2, [(0, acc)])
            dve.wait_ge(s["bias_done"], GROUPS)

            def add_bias(o, i):
                k = 8 * o + i
                e = dve.value_load(off_b[0:1, bass.ds(k, 1)], min_val=0, max_val=(E - 1) * HC)
                dve.wait_ge(s["ht2_ready"], k + 1)
                wait(dve, s["gelu_done"], k - 1)
                c4 = lambda m: m.rearrange("p (c n) -> p c n", c=HC)
                dve.tensor_tensor(c4(hb[:, i % 2, :]), c4(bank[3 + i % 2][:, :]), vec[:, bass.ds(e + R_FC, HC)].unsqueeze(2).broadcast_to([P, HC, P]), ALU.add).then_inc(s["hb_done"], 1)

            def y_out(o, i):
                k = 8 * o + i
                dve.wait_ge(s["y_ready"], k + 1)
                if i % 4 == 0:
                    wait(dve, s[f"st_done{i // 4}"], 16 * o)
                dve.tensor_copy(ys[:, i // 4, i % 4, :], bank[5 + i % 2][:, 0:D]).then_inc(s["ys_done"], 1)

            pipeline(dve, RT // 8, 8, [(0, add_bias), (2, y_out)])

            def rope(b, u):
                k = TB * b + u
                dve.wait_ge(s["raw_ready"], k + 1)
                wait(dve, s["o_ready"], k - 3)
                src = raw[:, u % 4, 0:256].rearrange("p (s h d) -> p s h d", s=2, h=NH)
                dst = qk[:, u % 4, :].rearrange("p (s h d) -> p s h d", s=2, h=NH)
                rt1, rt2 = rt1_r[:, u % 2], rt2_r[:, u % 2]
                wait(dve, s["roped"], k - 1)
                over = lambda m, n: m.unsqueeze(2).broadcast_to([P, 2, NH, n])
                dve.tensor_tensor(rt1[:, :, :, :], src[:, :, :, 0:ROT], over(ropec[:, u, :, :], ROT), ALU.mult)
                dve.tensor_tensor(rt2[:, :, :, 0::2], src[:, :, :, 1:ROT:2], over(ropes[:, u, :, 0::2], ROT // 2), ALU.mult)
                dve.tensor_tensor(rt2[:, :, :, 1::2], src[:, :, :, 0:ROT:2], over(ropes[:, u, :, 1::2], ROT // 2), ALU.mult).then_inc(s["rot_parts"], 1)
                dve.tensor_copy(dst[:, :, :, ROT:HD], src[:, :, :, ROT:HD])
                dve.wait_ge(s["rot_parts"], k + 1)
                dve.tensor_tensor(dst[:, :, :, 0:ROT], rt1[:, :, :, :], rt2[:, :, :, :], ALU.add).then_inc(s["roped"], 1)

            def mask(b, u):
                k = TB * b + u
                dve.wait_ge(s["st_ready"], k + 1)
                wait(dve, s["o_ready"], k - 3)
                dve.tensor_tensor(stm[:, u % 4, :, :], bank[4][:, 0:NH * P].rearrange("p (h n) -> p h n", h=NH),
                                  C["causal"].unsqueeze(1).broadcast_to([P, NH, P]), ALU.mult).then_inc(s["masked"], 1)

            def ret_out(b, u):
                k = TB * b + u
                dve.wait_ge(s["o_ready"], k + 1)
                dve.tensor_tensor(ret_all[:, bass.ds(k, 1), :].rearrange("p t (h d) -> p (t h) d", h=NH), bank[6 + u % 2][:, 0:D].rearrange("p (h d) -> p h d", h=NH),
                                  decq[:, u, :].unsqueeze(2).broadcast_to([P, NH, HD]), ALU.mult).then_inc(s["ret_done"], 1)

            def combine(b, u):
                k = TB * b + u
                dve.wait_ge(s[f"gath{u % 4}"], 32 * (2 * b + u // 4 + 1))
                x1 = x_all[:, bass.ds(k, 1), :].rearrange("p t d -> p (t d)")
                for j, g in enumerate((g1, g2)):
                    dve.scalar_tensor_tensor(x1, yg[:, u % 4, j, :], g[:, bass.ds(k, 1)], x1, ALU.mult, ALU.add).then_inc(s["part_sums" if j == 0 else "combined"], 1)
                    if j == 0:
                        dve.wait_ge(s["part_sums"], k + 1)

            pipeline(dve, B, TB, [(0, rope), (3, mask), (4, ret_out), (2, combine)])

            dve.wait_ge(s["ret_done"], TILES)
            for b in range(B):
                dve.tensor_reduce(gsum[:, NH * b:NH * (b + 1)], ret_all[:, TB * b:TB * (b + 1), :].rearrange("p t (h d) -> p h t d", h=NH), AX.XY, ALU.add).then_inc(s["gsum_ready"], 1)
            dve.wait_ge(s["gtot_ready"], 1)
            dve.tensor_scalar(gnm[:, :], bank[0][:, 0:NBH], -1.0 / (S * HD), None, ALU.mult).then_inc(s["gmean_ready"], 1)
            quarter = lambda m, b: m[:, b * 1024:(b + 1) * 1024]
            gate_f = gate_all[:, :, :].rearrange("p t d -> p (t d)")
            for b in range(B):
                dve.tensor_scalar(quarter(xnT, b), quarter(gate_f, b), 20.0, None, ALU.min).then_inc(s["mish_in"], 1)
            dve.wait_ge(s["gtot2_ready"], 1)
            dve.tensor_scalar(gva[:, :], bank[0][:, 0:NBH], 1.0 / (S * HD), EPS, ALU.mult, ALU.add).then_inc(s["gve_ready"], 1)
            for b in range(B):
                n, r, g = quarter(xnT, b), quarter(hT, b), quarter(gate_f, b)
                dve.wait_ge(s["mish_exp"], b + 1)
                link(dve.scalar_tensor_tensor(n, n, 2.0, n, ALU.add, ALU.mult))
                link(dve.tensor_scalar(r, n, 2.0, None, ALU.add))
                link(dve.reciprocal(r, r))
                link(dve.tensor_tensor(n, n, r, ALU.mult))
                link(dve.tensor_tensor(g, g, n, ALU.mult))
            dve.wait_ge(s["gr_ready"], 1)
            gwv = gn[:, 0:2].unsqueeze(1).broadcast_to([P, B, NH])
            gbv = gn[:, 2:4].unsqueeze(1).broadcast_to([P, B, NH])
            bh = lambda m: m.rearrange("p (b h) -> p b h", h=NH)
            link(dve.tensor_tensor(bh(gac[:, 0, :]), bh(gvb[:, :]), gwv, ALU.mult))
            link(dve.tensor_tensor(gva[:, :], gnm[:, :], gac[:, 0, :], ALU.mult))
            dve.tensor_tensor(bh(gac[:, 1, :]), bh(gva[:, :]), gbv, ALU.add).then_inc(s["gac_ready"], 1)

            def y_mul(o, i):
                k = 2 * o + i
                wait(dve, s["t1_ready"], k - 1)
                dve.wait_ge(s["yn_done"], k + 1)
                dve.tensor_tensor(hr[:, i, :, :], yn_r[:, i, :, :], gate_all[:, bass.ds(4 * k, 4), :], ALU.mult).then_inc(s["yr_done"], 1)

            def gate_ring(o, i):
                k = 2 * o + i
                wait(dve, s["tg_ready"], k - 1)
                dve.tensor_copy(gr[:, i, :, :], gate[:, bass.ds(4 * k, 4), :]).then_inc(s["gr_done"], 1)

            def y2(o, i):
                k = 2 * o + i
                g4 = gate_all[:, bass.ds(4 * k, 4), :]
                dve.wait_ge(s["wo_ready"], k + 1)
                dve.tensor_tensor(g4, bank[2][:, :].rearrange("p (t d) -> p t d", t=4), xn_all[:, bass.ds(4 * k, 4), :], ALU.add).then_inc(s["y2_done"], 1)
                dve.wait_ge(s["y2_done"], k + 1)
                moments(lambda u: gate_all[:, bass.ds(4 * k + u, 1), :].rearrange("p t d -> p (t d)"), i, k, "st2", "ag2", "ve2_ready")

            def z0(o, i):
                k = 2 * o + i
                dve.wait_ge(s["r2_ready"], k + 1)
                wait(dve, s["t2_ready"], k - 1)
                for u in range(4):
                    last = dve.tensor_scalar(xr[:, i, u, :], gate_all[:, bass.ds(4 * k + u, 1), :].rearrange("p t d -> p (t d)"),
                                             mv[:, i, u, 0:1], ra[:, i, u:u + 1], ALU.subtract, ALU.mult)
                last.then_inc(s["z0_done"], 1)
                x4 = x_all[:, bass.ds(4 * k, 4), :]
                dve.tensor_tensor(x4, x4, gate_all[:, bass.ds(4 * k, 4), :], ALU.add).then_inc(s["xy_done"], 1)

            def final(o, i):
                k = 2 * o + i
                dve.wait_ge(s["m2_ready"], k + 1)
                wait(dve, s[f"out_done{i}"], 16 * o)
                dve.wait_ge(s["xy_done"], k + 1)
                dve.tensor_tensor(ob[:, i, :, :], bank[5][:, :].rearrange("p (t d) -> p t d", t=4), x_all[:, bass.ds(4 * k, 4), :], ALU.add).then_inc(s["fin_ready"], 1)

            pipeline(dve, B, 2, [(0, y_mul), (1, y2), (2, z0), (3, gate_ring), (5, final)])


_INS = ["L0_attn_x", "L0_attn_ln1_w", "L0_attn_ln1_b", "L0_attn_wqkv_w", "L0_attn_wg_w", "L0_attn_wo_w", "L0_attn_gn_w", "L0_attn_gn_b",
        "L0_attn_ln2_w", "L0_attn_ln2_b", "L0_attn_w1_w", "L0_attn_w1_b", "L0_attn_w2_w", "L0_attn_w2_b", "L0_ffn_Wfc_s", "L0_ffn_bfc_s",
        "L0_ffn_Wproj_s", "L0_ffn_bproj_s", "L0_ffn_Wr", "L0_ffn_Wfc", "L0_ffn_bfc", "L0_ffn_Wproj", "L0_ffn_bproj"]


def kernel(**inputs):
    import concourse.bacc as bacc
    from concourse.bass_utils import run_bass_kernel_spmd

    nc = bacc.Bacc("TRN2", target_bir_lowering=False, num_devices=1)
    arrays, args = {}, {}
    for name in _INS:
        arrays[name] = np.ascontiguousarray(inputs[name])
        args[name] = nc.dram_tensor(name, arrays[name].shape, F32, kind="ExternalInput").ap()
    parts, cols, at = constants(), {}, 0
    for name, v in parts.items():
        cols[name] = (at, at + v.shape[1])
        at += v.shape[1]
    arrays["const"] = np.ascontiguousarray(np.concatenate(list(parts.values()), axis=1).astype(np.float32))
    const = nc.dram_tensor("const", arrays["const"].shape, F32, kind="ExternalInput").ap()
    out = nc.dram_tensor("out", (B, S, D), F32, kind="ExternalOutput").ap()
    build(nc, args, const, cols, out)
    return run_bass_kernel_spmd(nc, [arrays], core_ids=[0]).results[0]["out"]
```

```python
from contextlib import ExitStack

import numpy as np

import concourse.bass as bass
from concourse import mybir

ALU = mybir.AluOpType
ACT = mybir.ActivationFunctionType
AX = mybir.AxisListType
F32 = mybir.dt.float32
I32 = mybir.dt.int32

P = 128
B, S, D = 4, 1024, 128
TILES = B * S // P
GROUPS = TILES // 4
TB = S // P
NH, HD, ROT = 2, 64, 32
E, HID = 8, 512
HC = HID // P
EPS = 1e-5
BLOCKS = TILES * 2 // 4 + 2
RT = 4 * BLOCKS
NBH = B * NH


def constants():
    f4 = np.float32
    half = np.arange(0, ROT, 2, dtype=f4)
    inv_freq = (f4(1.0) / np.power(f4(10000.0), half / f4(ROT))).astype(f4)
    t = np.arange(S, dtype=f4)
    freqs = np.repeat((t[:, None] * inv_freq).astype(f4), 2, axis=-1).astype(np.float64)
    base = ((half + 0.4 * ROT) / (1.4 * ROT)).astype(np.float64)
    scale = base[None, :] ** ((t.astype(np.float64) - S // 2) / 512.0)[:, None]
    scale = np.concatenate((scale, scale), axis=-1)
    sign = np.where(np.arange(ROT) % 2 == 0, -1.0, 1.0)
    cos, sin = np.cos(freqs), np.sin(freqs) * sign
    both = lambda a: np.stack([a * scale, a / scale], 1)
    tiled = lambda a: a.reshape(TB, P, -1).transpose(1, 0, 2).reshape(P, -1)
    gamma = 1.0 - 2.0 ** (-5.0 - np.arange(NH))
    pos = np.arange(S, dtype=np.float64)[:, None]
    row = np.arange(P)
    full = lambda v: np.broadcast_to(np.asarray(v, np.float64), (P, len(v)))
    return {
        "ident": np.eye(P),
        "before": (row[:, None] < row[None, :]) * 1.0,
        "causal": (row[:, None] <= row[None, :]) * 1.0,
        "ones": np.ones((P, 256)),
        "heads": (row[:, None] == row[None, :] // HD) * 1.0,
        "head": (row[:, None] // HD == row[None, :] // HD) * 1.0,
        "mhalf": np.full((P, 8), -0.5),
        "eps": np.full((P, 4), EPS),
        "em8": full(np.arange(E) - E),
        "slot": full(np.arange(RT) * P),
        "ropec": tiled(both(cos)),
        "ropes": tiled(both(sin)),
        "deck": tiled(gamma[None, :] ** -pos),
        "decq": np.repeat(gamma[None, :] ** pos, HD, axis=1).T,
    }


def pipeline(eng, outer, inner, stages):
    longest = max(lag for lag, _ in stages)
    filled = (longest + 1) // inner + 1
    def step(o, i):
        for lag, fn in stages:
            oo, ii = o + (i - lag) // inner, (i - lag) % inner
            if not isinstance(oo, int) or 0 <= oo < outer:
                fn(oo, ii)

    for o in range(filled):
        for i in range(inner):
            step(o, i)
    if outer - filled == 1:
        filled, o = outer, outer - 1
        for i in range(inner):
            step(o, i)
    if filled < outer:
        with eng.Fori(filled, outer) as o:
            for i in range(inner):
                step(o, i)
    for i in range(longest):
        step(outer, i)


def by_group(fn):
    return lambda b, u: fn(2 * b + u // 4) if u % 4 == 3 else None


def by_sequence(fn):
    return lambda b, u: fn(b) if u == TB - 1 else None


def wait(eng, sem, n):
    if not isinstance(n, int) or n > 0:
        eng.wait_ge(sem, n)


def build(nc, a, const, cols, out):
    with ExitStack() as ctx:
        def sb(name, shape, dt=F32):
            return ctx.enter_context(nc.sbuf_tensor(name, shape, dt))

        def sem(name):
            return ctx.enter_context(nc.semaphore(name))

        bank = [ctx.enter_context(nc.psum_tensor(f"bank{i}", [P, 512], F32)) for i in range(2)]
        pair = ctx.enter_context(nc.psum_tensor("bank2_3", [P, 2, 512], F32))
        bank += [pair[:, 0, :], pair[:, 1, :]]
        bank += [ctx.enter_context(nc.psum_tensor(f"bank{i}", [P, 512], F32)) for i in range(4, 8)]

        slots_x = nc.dram_tensor("slots_x", (RT * P, D), F32, kind="Internal").ap()
        slots_y = nc.dram_tensor("slots_y", (RT * P, D), F32, kind="Internal").ap()

        cst = sb("cst", [P, const.shape[1]])
        C = {k: cst[:, lo:hi] for k, (lo, hi) in cols.items()}
        ident, ones = C["ident"], C["ones"]
        ropec = C["ropec"].rearrange("p (t s d) -> p t s d", t=TB, s=2)
        ropes = C["ropes"].rearrange("p (t s d) -> p t s d", t=TB, s=2)
        decq = C["decq"].rearrange("p (t n) -> p t n", t=TB)
        deck = C["deck"].rearrange("p (t h) -> p t h", t=TB)
        w_in = sb("w_in", [P, 384])
        wg = sb("wg", [P, D])
        wo, w1, w2 = sb("wo", [P, D]), sb("w1", [P, D]), sb("w2", [P, D])
        wr = sb("wr", [P, E])
        wfc_s, wproj_s = sb("wfc_s", [P, HID]), sb("wproj_s", [P, HC, D])
        wfc, wproj = sb("wfc", [P, E * HID]), sb("wproj", [P, E * HC * D])
        bproj = sb("bproj", [E, D])
        rows = sb("rows", [48, P])
        vec = sb("vec", [P, 48])
        out_rows = sb("out_rows", [2, D])
        out_bias = sb("out_bias", [P, D])
        gn_rows = sb("gn_rows", [NH, 2])
        gn = sb("gn", [P, 2])
        R_FC, R_FCS, R_L1W, R_L1B, R_L2W, R_L2B, R_W1B = 0, 32, 36, 37, 38, 39, 40
        N_ROWS = 41

        x_all = sb("x_all", [P, TILES, D])
        xn_all = sb("xn_all", [P, TILES, D])
        xnT = sb("xnT", [P, TILES * P])
        hT = sb("hT", [P, TILES * P])
        gate_all = sb("gate_all", [P, TILES * P])
        y2_all = gate_all[:, :].rearrange("p (t d) -> p t d", d=D)
        ret_all = sb("ret_all", [P, TILES * P])

        stats = sb("stats", [P, 2, 4, 6])
        mv = sb("mv", [P, 2, 4, 2])
        ve = sb("ve", [P, 2, 4])
        ra, rb, rc = sb("ra", [P, 2, 4]), sb("rb", [P, 2, 4]), sb("rc", [P, 4])
        xr, hr = sb("xr", [P, 2, 4, D]), sb("hr", [P, 2, 4, D])
        tr = sb("tr", [P, 2, 512])
        work = sb("work", [P, 4096])
        gs = work[:, :].rearrange("p (r c n) -> p r c n", r=2, c=HC)
        xin = work[:, 0:1024].rearrange("p (r u n) -> p r u n", r=2, u=4)
        hs = work[:, 1024:2048].rearrange("p (r n) -> p r n", r=2)
        hb = work[:, 2048:3072].rearrange("p (r n) -> p r n", r=2)
        gt = work[:, 3072:4096].rearrange("p (r n) -> p r n", r=2)
        xts = sb("xts", [P, 2, P])
        ys = sb("ys", [P, 2, 4, D])
        zeros = sb("zeros", [P, 256])
        raw = work[:, 0:1536].rearrange("p (r n) -> p r n", r=4)
        qk = work[:, 1536:2560].rearrange("p (r n) -> p r n", r=4)
        rt1_r, rt2_r = sb("rt1", [P, 2, 2, NH, ROT]), sb("rt2", [P, 2, 2, NH, ROT])
        vd = work[:, 2560:3072].rearrange("p (r n) -> p r n", r=4)
        kT = sb("kT", [P, 4, P])
        qT = sb("qT", [P, 4, P])
        stm = work[:, 3072:4096].rearrange("p (r h n) -> p r h n", r=4, h=NH)
        rs = sb("rs", [P, 4, D])
        yg = sb("yg", [P, 4, 2, D])
        ob = wfc[:, 3072:4096].rearrange("p (r u n) -> p r u n", r=2, u=4)
        lg = sb("lg", [P, TILES, E])
        oh1, oh2 = sb("oh1", [P, TILES, E]), sb("oh2", [P, TILES, E])
        spare = ret_all[:, :]
        ta, tb = (spare[:, j * 256:(j + 1) * 256].rearrange("p (t e) -> p t e", e=E) for j in range(2))
        m1, m2, im = sb("m1", [P, TILES]), sb("m2", [P, TILES]), sb("im", [P, TILES])
        dd, g1, g2 = sb("dd", [P, TILES]), sb("g1", [P, TILES]), sb("g2", [P, TILES])
        gate = sb("gate", [P, TILES, E])
        tot, cum, posn = (spare[:, j * 256:(j + 1) * 256].rearrange("p (e t) -> p e t", e=E) for j in range(2, 5))
        cnt, pad, endp, adj = (sb(n, [P, E]) for n in ("cnt", "pad", "endp", "adj"))
        cnti = sb("cnti", [P, E], I32)
        idx1, idx2 = sb("idx1", [P, TILES], I32), sb("idx2", [P, TILES], I32)
        ended = ret_all[0:1, 1280:1280 + RT * E].rearrange("p (j e) -> p j e", e=E)
        tile_e = sb("tile_e", [1, RT])
        off_w, off_b = sb("off_w", [1, RT], I32), sb("off_b", [1, RT], I32)
        gsum, gsq, gnm, gva, gvb, gna, gnc = (sb(n, [P, B]) for n in ("gsum", "gsq", "gnm", "gva", "gvb", "gna", "gnc"))
        squares = wproj[:, 0:2048].rearrange("p (r n) -> p r n", r=2)
        yn_r = wproj[:, 2048:3072].rearrange("p (r n) -> p r n", r=2)
        yT, zT, aT = (wfc[:, j * 1024:(j + 1) * 1024].rearrange("p (r n) -> p r n", r=2) for j in range(3))
        gT = sb("gT", [E, 2, 512])

        names = """tables_in cst_in vec_in win_in wr_in wshared_in wexp_in watt_in zero_in x_in0 x_in1 xn_kept0 xn_kept1 zeroed pre_pe pre_act ve_ready r_ready
            xn_done tr_ready xnt_done ht_done lg_ready link_v link_p mask_ready rank_ready dd_ready ex_ready idx_ready off_ready scattered
            fc_ready gs_done proj_ready acc_done xs_in0 xs_in1 xt_ready xt_copied h_ready hs_copied ht2_ready hb_done gelu_done y_ready
            ys_done st_done0 st_done1 roped vd_done qkt_ready st_ready state_ready o_ready gath0 gath1 gath2 gath3 combined gsum_ready
            gtot_ready gmean_ready gsq_ready gtot2_ready gve_ready gr_ready gac_ready mish_exp rsq sp_passed stats_landed st1 ag1 st2 ag2
            bias_done rot_parts part_sums xy_done yn_done tg_ready wo_ready ve2_ready r2_ready z0_done t2_ready m1_ready m2_ready fin_ready
            out_done0 out_done1 clamped const drained0 drained1 drained2 drained4 drained5 drained6 drained7 g_kept g_ready gna_ready
            mish_steps qkv_ready rs_zero yt_done""".split()
        s = {n: sem(n) for n in names}
        block = ctx.enter_context(nc.Block())

        x_d = a["L0_attn_x"].rearrange("b (t p) d -> p (b t) d", p=P)
        out_d = out.rearrange("b (t p) d -> p (b t) d", p=P)
        one_row = lambda v: v.rearrange("(o n) -> o n", o=1)

        @block.sync
        def _(sp):
            def sp_wait(sem, n):
                wait(sp, sem, n)
                if not isinstance(n, int):
                    sp.sem_inc(s["sp_passed"], 1)

            def load_x(o, i):
                n, t = 16 * o, 8 * o + 4 * i
                sp_wait(s[f"x_in{i}"], n)
                sp.dma_start(x_all[:, bass.ds(t, 4), :], x_d[:, bass.ds(t, 4), :]).then_inc(s[f"x_in{i}"], 16)

            def keep_xn(o, i):
                done, n, t = 2 * o + i + 1, 16 * o, 8 * o + 4 * i
                sp_wait(s["xn_done"], done)
                sp_wait(s[f"xn_kept{i}"], n)
                sp.dma_start(xn_all[:, bass.ds(t, 4), :], xr[:, i, :, :]).then_inc(s[f"xn_kept{i}"], 16)

            load_x(0, 0)
            late = cols["ropec"][0]
            sp.dma_start(cst[:, 0:late], const[:, 0:late]).then_inc(s["cst_in"], 16)
            load_x(0, 1)
            for i, v in enumerate((a["L0_attn_ln1_w"], a["L0_attn_ln1_b"], a["L0_attn_ln2_w"], a["L0_attn_ln2_b"], a["L0_attn_w1_b"])):
                sp.dma_start(rows[R_L1W + i:R_L1W + i + 1, :], one_row(v)).then_inc(s["vec_in"], 16)
            sp.dma_start(rows[R_FC:R_FC + E * HC, :], a["L0_ffn_bfc"].rearrange("e (c p) -> (e c) p", p=P)).then_inc(s["vec_in"], 16)
            sp.dma_start(rows[R_FCS:R_FCS + HC, :], a["L0_ffn_bfc_s"].rearrange("(c p) -> c p", p=P)).then_inc(s["vec_in"], 16)
            sp.dma_start(out_rows[0:1, :], one_row(a["L0_attn_w2_b"])).then_inc(s["vec_in"], 16)
            sp.dma_start(out_rows[1:2, :], one_row(a["L0_ffn_bproj_s"])).then_inc(s["vec_in"], 16)
            sp.dma_start(gn_rows[:, 0:1], a["L0_attn_gn_w"].rearrange("(n o) -> n o", o=1)).then_inc(s["vec_in"], 16)
            sp.dma_start(gn_rows[:, 1:2], a["L0_attn_gn_b"].rearrange("(n o) -> n o", o=1)).then_inc(s["vec_in"], 16)
            sp.dma_start(wr[:, :], a["L0_ffn_Wr"]).then_inc(s["wr_in"], 16)
            pipeline(sp, 4, 2, [(0, lambda o, i: load_x(o, i) if not isinstance(o, int) or o else None), (2, keep_xn)])
            sp.wait_ge(s["zero_in"], 1)
            sp.dma_start(slots_x.rearrange("(p q n) d -> p q (n d)", p=P, n=2), zeros[:, :].unsqueeze(1).broadcast_to([P, RT // 2, 256])).then_inc(s["zeroed"], 16)
            sp.dma_start(wfc_s[:, :], a["L0_ffn_Wfc_s"]).then_inc(s["wshared_in"], 16)
            sp.dma_start(wproj_s[:, :, :], a["L0_ffn_Wproj_s"].rearrange("(c p) d -> p c d", p=P)).then_inc(s["wshared_in"], 16)
            sp.dma_start(wg[:, :], a["L0_attn_wg_w"]).then_inc(s["wshared_in"], 16)
            sp.dma_start(wfc[:, :].rearrange("p (e n) -> p e n", e=E), a["L0_ffn_Wfc"].rearrange("e p n -> p e n")).then_inc(s["wexp_in"], 16)
            sp.dma_start(wproj[:, :].rearrange("p (e c d) -> p e c d", e=E, c=HC), a["L0_ffn_Wproj"].rearrange("e (c p) d -> p e c d", p=P)).then_inc(s["wexp_in"], 16)
            for h in range(NH):
                sp.dma_start(w_in[:, :].rearrange("p (s h d) -> p s h d", s=3, h=NH)[:, :, h, :],
                             a["L0_attn_wqkv_w"].rearrange("p (h s d) -> p s h d", h=NH, s=3)[:, :, h, :]).then_inc(s["win_in"], 16)
            sp.dma_start(cst[:, late:], const[:, late:]).then_inc(s["tables_in"], 16)
            for w, v in ((wo, "wo"), (w1, "w1"), (w2, "w2")):
                sp.dma_start(w[:, :], a[f"L0_attn_{v}_w"]).then_inc(s["watt_in"], 16)
            sp.dma_start(bproj[:, :], a["L0_ffn_bproj"]).then_inc(s["watt_in"], 16)

            def load_slots(o, i):
                read, n, q = 8 * o + 4 * i - 4, 16 * o, 2 * o + i
                sp_wait(s["xt_ready"], read)
                sp_wait(s[f"xs_in{i}"], n)
                sp.dma_start(xin[:, i, :, :], slots_x.rearrange("(q u p) d -> q p u d", u=4, p=P)[bass.ds(q, 1)].rearrange("q p u d -> p (q u) d")).then_inc(s[f"xs_in{i}"], 16)

            def store_slots(o, i):
                done, n, q = 8 * o + 4 * i + 4, 16 * o, 2 * o + i
                sp_wait(s["ys_done"], done)
                sp_wait(s[f"st_done{i}"], n)
                sp.dma_start(slots_y.rearrange("(q u p) d -> q p u d", u=4, p=P)[bass.ds(q, 1)].rearrange("q p u d -> p (q u) d"), ys[:, i, :, :]).then_inc(s[f"st_done{i}"], 16)

            sp.wait_ge(s["scattered"], 16 * 2 * TILES)
            sp.wait_ge(s["proj_ready"], GROUPS)
            pipeline(sp, BLOCKS // 2, 2, [(0, load_slots), (2, store_slots)])

            def store_out(o, i):
                done, n, t = 2 * o + i + 1, 16 * o, 8 * o + 4 * i
                sp_wait(s["fin_ready"], done)
                sp_wait(s[f"out_done{i}"], n)
                sp.dma_start(out_d[:, bass.ds(t, 4), :], ob[:, i, :, :]).then_inc(s[f"out_done{i}"], 16)

            pipeline(sp, B, 2, [(0, store_out)])
            sp.wait_ge(s["out_done0"], 16 * B)
            sp.wait_ge(s["out_done1"], 16 * B)

        @block.tensor
        def _(pe):
            pe.wait_ge(s["cst_in"], 16)
            pe.wait_ge(s["vec_in"], 16 * 11)
            pe.transpose(bank[5][:, 0:N_ROWS], rows[0:N_ROWS, :], ident[0:N_ROWS, 0:N_ROWS])
            pe.matmul(bank[6][:, 0:D], ones[0:2, 0:P], out_rows[:, :], start=True, stop=True)
            pe.matmul(bank[6][:, D:D + 2], C["heads"][0:NH, :], gn_rows[:, :], start=True, stop=True).then_inc(s["pre_pe"], 1)
            pe.wait_ge(s["wr_in"], 16)

            def p1_transpose(o, i):
                k = 2 * o + i
                pe.wait_ge(s["xn_done"], k + 1)
                wait(pe, s["ht_done"], k - 1)
                for u in range(4):
                    pe.transpose(bank[i][:, u * P:(u + 1) * P], xr[:, i, u, :], ident)
                for u in range(4):
                    last = pe.transpose(bank[2 + i][:, u * P:(u + 1) * P], hr[:, i, u, :], ident)
                last.then_inc(s["tr_ready"], 1)

            def p1_logits(o, i):
                k = 2 * o + i
                pe.wait_ge(s["xnt_done"], k + 1)
                for u in range(4):
                    last = pe.matmul(bank[4][:, bass.ds(k * 4 * E + u * E, E)], tr[:, i, u * P:(u + 1) * P], wr[:, :], start=True, stop=True)
                last.then_inc(s["lg_ready"], 1)

            pipeline(pe, 4, 2, [(0, p1_transpose), (1, p1_logits)])

            def ranks():
                pe.wait_ge(s["mask_ready"], 1)
                pe.matmul(bank[5][:, 0:256], C["before"], ta[:, :, :].rearrange("p t e -> p (t e)"), start=True, stop=True)
                pe.matmul(bank[6][:, 0:256], ones[:, 0:P], ta[:, :, :].rearrange("p t e -> p (t e)"), start=True, stop=True).then_inc(s["rank_ready"], 1)

            def fc(o, i):
                k = 2 * o + i
                for c in range(HC):
                    wait(pe, s["gs_done"], HC * (k - 1) + c + 1)
                    pe.matmul(bank[c][:, :], wfc_s[:, c * P:(c + 1) * P], xnT[:, bass.ds(k * 512, 512)], start=True, stop=True).then_inc(s["fc_ready"], 1)
                wait(pe, s["clamped"], k)
                pe.matmul(bank[4][:, :], wg[:, :], hT[:, bass.ds(k * 512, 512)], start=True, stop=True).then_inc(s["g_ready"], 1)

            def proj(o, i):
                k = 2 * o + i
                pe.wait_ge(s["gs_done"], HC * (k + 1))
                wait(pe, s["acc_done"], k)
                for u in range(4):
                    for c in range(HC):
                        last = pe.matmul(bank[7][:, u * P:(u + 1) * P], gs[:, i, c, u * P:(u + 1) * P], wproj_s[:, c, :], start=(c == 0), stop=(c == HC - 1))
                last.then_inc(s["proj_ready"], 1)

            pe.wait_ge(s["wshared_in"], 48)
            pe.wait_ge(s["ht_done"], GROUPS)
            ranks()
            pipeline(pe, 4, 2, [(0, fc), (1, proj)])

            pe.wait_ge(s["off_ready"], 1)
            pe.wait_ge(s["wexp_in"], 32)
            pe.wait_ge(s["acc_done"], GROUPS)

            def expert(o, i):
                return pe.value_load(off_w[0:1, bass.ds(8 * o + i, 1)], min_val=0, max_val=(E - 1) * HID)

            def x_transpose(o, i):
                k = 8 * o + i
                if i % 4 == 0:
                    pe.wait_ge(s[f"xs_in{i // 4}"], 16 * (o + 1))
                wait(pe, s["xt_copied"], k)
                pe.transpose(bank[0][:, 0:P], xin[:, i // 4, i % 4, :], ident).then_inc(s["xt_ready"], 1)

            def up(o, i):
                k = 8 * o + i
                e = expert(o, i)
                pe.wait_ge(s["xt_copied"], k + 1)
                wait(pe, s["hs_copied"], k - 1)
                pe.matmul(bank[1 + i % 2][:, :], xts[:, i % 2, :], wfc[:, bass.ds(e, HID)], start=True, stop=True).then_inc(s["h_ready"], 1)

            def h_transpose(o, i):
                k = 8 * o + i
                pe.wait_ge(s["hs_copied"], k + 1)
                wait(pe, s["hb_done"], k - 1)
                for c in range(HC):
                    last = pe.transpose(bank[3 + i % 2][:, c * P:(c + 1) * P], hs[:, i % 2, c * P:(c + 1) * P], ident)
                last.then_inc(s["ht2_ready"], 1)

            def down(o, i):
                k = 8 * o + i
                e = expert(o, i)
                pe.wait_ge(s["gelu_done"], k + 1)
                wait(pe, s["ys_done"], k - 1)
                for c in range(HC):
                    last = pe.matmul(bank[5 + i % 2][:, 0:D], gt[:, i % 2, c * P:(c + 1) * P], wproj[:, bass.ds(e + c * D, D)], start=(c == 0), stop=(c == HC - 1))
                last.then_inc(s["y_ready"], 1)

            pipeline(pe, RT // 8, 8, [(0, x_transpose), (1, up), (4, down), (2, h_transpose)])

            pe.wait_ge(s["win_in"], 32)
            pe.wait_ge(s["watt_in"], 64)
            pe.wait_ge(s["ys_done"], RT)
            pe.wait_ge(s["rs_zero"], 1)
            used = dict.fromkeys(range(8), 0)

            def take(n):
                wait(pe, s[f"drained{n}"], used[n])
                used[n] += 1

            def project(b, u):
                k = TB * b + u
                take(0)
                pe.matmul(bank[0][:, 0:384], hT[:, k * P:(k + 1) * P], w_in[:, :], start=True, stop=True).then_inc(s["qkv_ready"], 1)

            def qk_transpose(b, u):
                k = TB * b + u
                pe.wait_ge(s["roped"], k + 1)
                take(1)
                for j in range(2):
                    last = pe.transpose(bank[1][:, j * P:(j + 1) * P], qk[:, u % 4, j * P:(j + 1) * P], ident)
                last.then_inc(s["qkt_ready"], 1)

            def scores(b, u):
                k = TB * b + u
                pe.wait_ge(s["drained1"], k + 1)
                take(2)
                for h in range(NH):
                    hp = slice(h * HD, (h + 1) * HD)
                    last = pe.matmul(pair[:, h, 0:P], kT[hp, u % 4, :], qT[hp, u % 4, :], start=True, stop=True)
                last.then_inc(s["st_ready"], 1)
                pe.wait_ge(s["vd_done"], k + 1)
                take(4)
                pe.matmul(bank[4][:, 0:D], qk[:, u % 4, P:2 * P], vd[:, u % 4, :], start=(u == 0), stop=True, skip_group_check=True).then_inc(s["state_ready"], 1)

            def outputs(b, u):
                k = TB * b + u
                pe.wait_ge(s["drained2"], k + 1)
                wait(pe, s["drained4"], k)
                take(5)
                if u > 0:
                    pe.matmul(bank[5][:, 0:P], rs[:, (u - 1) % 4, :], qT[:, u % 4, :], start=True, stop=False, skip_group_check=True)
                for h in range(NH):
                    hp = slice(h * HD, (h + 1) * HD)
                    last = pe.matmul(bank[5][hp, 0:P], vd[:, u % 4, hp], stm[:, u % 4, h, :], start=(u == 0), stop=True, skip_group_check=True)
                last.then_inc(s["o_ready"], 1)

            def norm_sum(b, src, ready, done):
                pe.wait_ge(s[ready], b + 1)
                take(7)
                pe.matmul(bank[7][:, 0:1], C["head"], src[:, b:b + 1], start=True, stop=True).then_inc(s[done], 1)

            def wo_mm(k):
                pe.wait_ge(s["yt_done"], k + 1)
                take(6)
                for v in range(4):
                    last = pe.matmul(bank[6][:, v * P:(v + 1) * P], yT[:, k % 2, v * P:(v + 1) * P], wo[:, :], start=True, stop=True)
                last.then_inc(s["wo_ready"], 1)

            def z_transpose(k):
                pe.wait_ge(s["z0_done"], k + 1)
                take(6)
                for v in range(4):
                    last = pe.transpose(bank[6][:, v * P:(v + 1) * P], xr[:, k % 2, v, :], ident)
                last.then_inc(s["t2_ready"], 1)

            def w1_mm(k):
                pe.wait_ge(s["drained6"], 2 * k + 2)
                take(7)
                pe.matmul(bank[7][:, :], w1[:, :], zT[:, k % 2, :], start=True, stop=True).then_inc(s["m1_ready"], 1)
                take(7)
                for v in range(4):
                    last = pe.transpose(bank[7][0:E, v * P:(v + 1) * P], gate[:, 4 * k + v, :], ident)
                last.then_inc(s["tg_ready"], 1)

            def w2_mm(k):
                take(7)
                for v in range(4):
                    pe.matmul(bank[7][:, v * P:(v + 1) * P], aT[:, k % 2, v * P:(v + 1) * P], w2[:, :], start=True, stop=False)
                    last = pe.matmul(bank[7][:, v * P:(v + 1) * P], gT[:, k % 2, v * P:(v + 1) * P], bproj[:, :], start=False, stop=True)
                last.then_inc(s["m2_ready"], 1)

            pipeline(pe, B, TB, [(0, project), (2, qk_transpose), (4, outputs), (3, scores),
                                 (5, by_sequence(lambda b: norm_sum(b, gsum, "gsum_ready", "gtot_ready"))),
                                 (7, by_sequence(lambda b: norm_sum(b, gsq, "gsq_ready", "gtot2_ready"))),
                                 (14, by_group(wo_mm)), (16, by_group(z_transpose)), (17, by_group(w1_mm)), (18, by_group(w2_mm))])

        @block.scalar
        def _(act):
            act.wait_ge(s["pre_pe"], 1)
            act.activation(vec[:, 0:N_ROWS], bank[5][:, 0:N_ROWS], ACT.Copy)
            act.activation(out_bias[:, :], bank[6][:, 0:D], ACT.Copy)
            act.activation(gn[:, :], bank[6][:, D:D + 2], ACT.Copy).then_inc(s["pre_act"], 1)
            act.wait_ge(s["pre_act"], 1)

            def p1_copy(o, i):
                k = 2 * o + i
                act.wait_ge(s["tr_ready"], k + 1)
                wait(act, s["lg_ready"], k - 1)
                act.activation(tr[:, i, :], bank[i][:, :], ACT.Copy).then_inc(s["xnt_done"], 1)
                act.activation(xnT[:, bass.ds(k * 512, 512)], bank[i][:, :], ACT.Copy)
                act.activation(hT[:, bass.ds(k * 512, 512)], bank[2 + i][:, :], ACT.Identity, bias=vec[:, R_L1B:R_L1B + 1], scale=vec[:, R_L1W:R_L1W + 1]).then_inc(s["ht_done"], 1)

            pipeline(act, 4, 2, [(0, p1_copy)])
            act.wait_ge(s["dd_ready"], 1)
            act.activation(g2[:, :], dd[:, :], ACT.Exp).then_inc(s["ex_ready"], 1)

            def shared_gelu(o, i):
                k = 2 * o + i
                wait(act, s["proj_ready"], k - 1)
                for c in range(HC):
                    act.wait_ge(s["fc_ready"], HC * k + c + 1)
                    act.activation(gs[:, i, c, :], bank[c][:, :], ACT.Gelu_apprx_tanh, bias=vec[:, R_FCS + c:R_FCS + c + 1]).then_inc(s["gs_done"], 1)

            pipeline(act, 4, 2, [(0, shared_gelu)])
            act.wait_ge(s["clamped"], GROUPS)
            act.activation(xnT[:, :], xnT[:, :], ACT.Exp).then_inc(s["mish_exp"], 1)
            act.wait_ge(s["proj_ready"], GROUPS)

            def xt_copy(o, i):
                k = 8 * o + i
                act.wait_ge(s["xt_ready"], k + 1)
                wait(act, s["h_ready"], k - 1)
                act.activation(xts[:, i % 2, :], bank[0][:, 0:P], ACT.Copy).then_inc(s["xt_copied"], 1)

            def h_copy(o, i):
                k = 8 * o + i
                act.wait_ge(s["h_ready"], k + 1)
                wait(act, s["ht2_ready"], k - 1)
                act.activation(hs[:, i % 2, :], bank[1 + i % 2][:, :], ACT.Copy).then_inc(s["hs_copied"], 1)

            def gelu(o, i):
                k = 8 * o + i
                act.wait_ge(s["hb_done"], k + 1)
                wait(act, s["y_ready"], k - 1)
                act.activation(gt[:, i % 2, :], hb[:, i % 2, :], ACT.Gelu_apprx_tanh).then_inc(s["gelu_done"], 1)

            pipeline(act, RT // 8, 8, [(0, xt_copy), (1, h_copy), (2, gelu)])

            act.wait_ge(s["rs_zero"], 1)

            def qkv_copy(b, u):
                k = TB * b + u
                act.wait_ge(s["qkv_ready"], k + 1)
                wait(act, s["roped"], k - 3)
                wait(act, s["vd_done"], k - 3)
                act.activation(raw[:, u % 4, :], bank[0][:, 0:384], ACT.Copy).then_inc(s["drained0"], 1)

            def kt_copy(b, u):
                k = TB * b + u
                act.wait_ge(s["qkt_ready"], k + 1)
                wait(act, s["o_ready"], k - 3)
                act.activation(qT[:, u % 4, :], bank[1][:, 0:P], ACT.Copy)
                act.activation(kT[:, u % 4, :], bank[1][:, P:2 * P], ACT.Copy).then_inc(s["drained1"], 1)

            def r_copy(b, u):
                k = TB * b + u
                act.wait_ge(s["state_ready"], k + 1)
                wait(act, s["o_ready"], k - 2)
                for h in range(NH):
                    hp = slice(h * HD, (h + 1) * HD)
                    last = act.activation(rs[hp, u % 4, hp], bank[4][hp, hp], ACT.Copy)
                last.then_inc(s["drained4"], 1)

            def norm_first(b):
                act.wait_ge(s["drained5"], TB * (b + 1))
                wait(act, s["gsq_ready"], b)
                act.activation(squares[:, 0, :], ret_all[:, b * S:(b + 1) * S], ACT.Copy, accum_out=gsum[:, b:b + 1]).then_inc(s["gsum_ready"], 1)

            def norm_second(b):
                act.wait_ge(s["gmean_ready"], b + 1)
                act.activation(squares[:, 1, :], ret_all[:, b * S:(b + 1) * S], ACT.Square, bias=gnm[:, b:b + 1], accum_out=gsq[:, b:b + 1]).then_inc(s["gsq_ready"], 1)

            def yn(k):
                act.wait_ge(s["gac_ready"], k // 2 + 1)
                wait(act, s["yt_done"], k - 1)
                act.activation(yn_r[:, k % 2, :], ret_all[:, k * 512:(k + 1) * 512], ACT.Identity,
                               bias=gnc[:, k // 2:k // 2 + 1], scale=gna[:, k // 2:k // 2 + 1]).then_inc(s["yn_done"], 1)

            def z_copy(k):
                act.wait_ge(s["t2_ready"], k + 1)
                wait(act, s["m1_ready"], k - 1)
                act.activation(zT[:, k % 2, :], bank[6][:, :], ACT.Identity, bias=vec[:, R_L2B:R_L2B + 1], scale=vec[:, R_L2W:R_L2W + 1]).then_inc(s["drained6"], 1)

            def ffn_gelu(k):
                act.wait_ge(s["m1_ready"], k + 1)
                wait(act, s["m2_ready"], k - 1)
                act.activation(aT[:, k % 2, :], bank[7][:, :], ACT.Gelu, bias=vec[:, R_W1B:R_W1B + 1]).then_inc(s["drained7"], 1)
                act.wait_ge(s["tg_ready"], k + 1)
                act.activation(gT[:, k % 2, :], bank[7][0:E, :], ACT.Copy).then_inc(s["drained7"], 1)

            pipeline(act, B, TB, [(0, qkv_copy), (2, kt_copy), (3, r_copy), (5, by_sequence(norm_first)), (6, by_sequence(norm_second)),
                                  (13, by_group(yn)), (16, by_group(z_copy)), (17, by_group(ffn_gelu))])

        @block.gpsimd
        def _(pool):
            pool.memset(zeros[:, :], 0.0).then_inc(s["zero_in"], 1)
            pool.memset(rs[:, :, :], 0.0).then_inc(s["rs_zero"], 1)
            pool.wait_ge(s["cst_in"], 16)
            chain = [0]

            def link(ins):
                chain[0] += 1
                ins.then_inc(s["link_p"], 1)
                pool.wait_ge(s["link_p"], chain[0])

            def rsqrt(o, i):
                k = 2 * o + i
                n = 5 * k
                pool.wait_ge(s["ve_ready"], k + 1)
                wait(pool, s["xn_done"], k - 1)
                v = mv[:, i, :, 1]
                steps = (
                    lambda: pool.tensor_tensor(ra[:, i, :], ve[:, i, :], C["mhalf"][:, 0:4], ALU.pow),
                    lambda: pool.tensor_tensor(rb[:, i, :], v, ra[:, i, :], ALU.mult),
                    lambda: pool.tensor_tensor(rb[:, i, :], rb[:, i, :], ra[:, i, :], ALU.mult),
                    lambda: pool.tensor_tensor(rc[:, :], rb[:, i, :], C["eps"], ALU.add),
                    lambda: pool.tensor_tensor(rb[:, i, :], rc[:, :], C["mhalf"][:, 0:4], ALU.pow),
                )
                for j, f in enumerate(steps):
                    f().then_inc(s["rsq"], 1)
                    pool.wait_ge(s["rsq"], n + j + 1)
                pool.tensor_tensor(rb[:, i, :], rb[:, i, :], ra[:, i, :], ALU.mult).then_inc(s["r_ready"], 1)

            pipeline(pool, 4, 2, [(0, rsqrt)])

            pool.wait_ge(s["idx_ready"], 1)
            for i in range(2):
                pool.wait_ge(s[f"xn_kept{i}"], 16 * 4)
            pool.wait_ge(s["zeroed"], 16)
            for t in range(TILES):
                for idx in (idx1, idx2):
                    pool.indirect_dma_start(out=slots_x, out_offset=bass.IndirectOffsetOnAxis(ap=idx[:, t:t + 1], axis=0),
                                            in_=xn_all[:, t, :], in_offset=None).then_inc(s["scattered"], 16)

            def norms_after(t):
                if t % TB == 7 and TB < t <= TB * (B + 1):
                    b = t // TB - 1
                    pool.wait_ge(s["gve_ready"], b + 1)
                    pool.tensor_tensor(gvb[:, b:b + 1], gva[:, b:b + 1], C["mhalf"][:, 0:1], ALU.pow).then_inc(s["gr_ready"], 1)
                if t % 4 == 2 and 0 <= (t - 18) // 4 < GROUPS:
                    k = (t - 18) // 4
                    pool.wait_ge(s["ve2_ready"], k + 1)
                    pool.tensor_tensor(ra[:, k % 2, :], ve[:, k % 2, :], C["mhalf"][:, 0:4], ALU.pow).then_inc(s["r2_ready"], 1)

            for i in range(2):
                pool.wait_ge(s[f"st_done{i}"], 16 * BLOCKS // 2)
            pool.wait_ge(s["tables_in"], 16)
            for t in range(TILES):
                u = t % TB
                if t >= 4:
                    pool.wait_ge(s["combined"], t - 3)
                for j, idx in enumerate((idx1, idx2)):
                    pool.indirect_dma_start(out=yg[:, t % 4, j, :], out_offset=None, in_=slots_y,
                                            in_offset=bass.IndirectOffsetOnAxis(ap=idx[:, t:t + 1], axis=0)).then_inc(s[f"gath{t % 4}"], 16)
                pool.wait_ge(s["drained0"], t + 1)
                if t >= 4:
                    pool.wait_ge(s["o_ready"], t - 3)
                pool.tensor_tensor(vd[:, t % 4, :].rearrange("p (h d) -> p h d", h=NH), raw[:, t % 4, 256:384].rearrange("p (h d) -> p h d", h=NH),
                                   deck[:, u, :].unsqueeze(2).broadcast_to([P, NH, HD]), ALU.mult).then_inc(s["vd_done"], 1)

                norms_after(t)
            for t in range(TILES, TILES + 16):
                norms_after(t)

        @block.vector
        def _(dve):
            chain = [0]

            def link(ins):
                chain[0] += 1
                ins.then_inc(s["link_v"], 1)
                dve.wait_ge(s["link_v"], chain[0])

            def moments(x4, i, k, stat, aggr, ready):
                for u in range(4):
                    last = dve.bn_stats(stats[:, i, u, :], x4(u))
                last.then_inc(s[stat], 1)
                dve.wait_ge(s[stat], k + 1)
                dve.sem_inc(s["stats_landed"], 1)
                for u in range(4):
                    last = dve.bn_aggr(mv[:, i, u, :], stats[:, i, u, :])
                last.then_inc(s[aggr], 1)
                dve.wait_ge(s[aggr], k + 1)
                dve.tensor_scalar(ve[:, i, :], mv[:, i, :, 1], EPS, None, ALU.add).then_inc(s[ready], 1)

            def p1_moments(o, i):
                k = 2 * o + i
                dve.wait_ge(s[f"x_in{i}"], 16 * (o + 1))
                moments(lambda u: x_all[:, bass.ds(4 * k + u, 1), :].rearrange("p t d -> p (t d)"), i, k, "st1", "ag1", "ve_ready")

            def p1_norm(o, i):
                k = 2 * o + i
                dve.wait_ge(s["r_ready"], k + 1)
                wait(dve, s[f"xn_kept{i}"], 16 * o)
                wait(dve, s["tr_ready"], k - 1)
                for r, ring in ((ra, xr), (rb, hr)):
                    for u in range(4):
                        last = dve.tensor_scalar(ring[:, i, u, :], x_all[:, bass.ds(4 * k + u, 1), :].rearrange("p t d -> p (t d)"),
                                                 mv[:, i, u, 0:1], r[:, i, u:u + 1], ALU.subtract, ALU.mult)
                last.then_inc(s["xn_done"], 1)

            pipeline(dve, 4, 2, [(0, p1_moments), (1, p1_norm)])

            em8 = C["em8"].unsqueeze(1).broadcast_to([P, TILES, E])
            wide = lambda m: m[:, :].unsqueeze(2).broadcast_to([P, TILES, E])
            by_e = lambda m: m.rearrange("p t e -> p e t")
            dve.wait_ge(s["lg_ready"], GROUPS)
            link(dve.tensor_copy(lg[:, :, :].rearrange("p t e -> p (t e)"), bank[4][:, 0:256]))
            for m, oh in ((m1, oh1), (m2, oh2)):
                src = lg if m is m1 else tb
                link(dve.tensor_reduce(m[:, :], src[:, :, :], AX.X, ALU.max))
                link(dve.tensor_tensor(ta[:, :, :], src[:, :, :], wide(m), ALU.is_equal))
                link(dve.tensor_tensor(ta[:, :, :], ta[:, :, :], em8, ALU.mult))
                link(dve.tensor_reduce(im[:, :], ta[:, :, :], AX.X, ALU.min))
                link(dve.tensor_tensor(oh[:, :, :], em8, wide(im), ALU.is_equal))
                if m is m1:
                    link(dve.scalar_tensor_tensor(tb[:, :, :], oh[:, :, :], -3e38, lg[:, :, :], ALU.mult, ALU.add))
            dve.tensor_tensor(ta[:, :, :], oh1[:, :, :], oh2[:, :, :], ALU.add).then_inc(s["mask_ready"], 1)
            dve.tensor_tensor(dd[:, :], m2[:, :], m1[:, :], ALU.subtract).then_inc(s["dd_ready"], 1)
            dve.wait_ge(s["rank_ready"], 1)
            link(dve.tensor_copy(tot[:, :, :], by_e(bank[6][:, 0:256].rearrange("p (t e) -> p t e", e=E))))
            flat = lambda m: m[:, :, :].rearrange("p e t -> p (e t)")
            link(dve.tensor_tensor_scan(flat(cum), C["ones"], flat(tot), 0.0, ALU.mult, ALU.add))
            link(dve.tensor_copy(cnt[:, :], cum[:, :, TILES - 1]))
            link(dve.tensor_tensor(pad[:, 1:E], cnt[:, 1:E], cnt[:, 0:E - 1], ALU.subtract))
            link(dve.tensor_copy(pad[:, 0:1], cnt[:, 0:1]))
            link(dve.tensor_scalar(cnti[:, :], pad[:, :], float(P - 1), None, ALU.add))
            link(dve.tensor_scalar(cnti[:, :], cnti[:, :], 7, 7, ALU.logical_shift_right, ALU.logical_shift_left))
            link(dve.tensor_tensor(adj[:, :], cnt[:, :], pad[:, :], ALU.subtract))
            link(dve.tensor_copy(pad[:, :], cnti[:, :]))
            link(dve.tensor_tensor_scan(endp[:, :], C["ones"][:, 0:E], pad[:, :], 0.0, ALU.mult, ALU.add))
            link(dve.tensor_tensor(pad[:, :], endp[:, :], pad[:, :], ALU.subtract))
            link(dve.tensor_tensor(adj[:, :], pad[:, :], adj[:, :], ALU.subtract))
            link(dve.tensor_tensor(posn[:, :, :], cum[:, :, :], tot[:, :, :], ALU.subtract))
            link(dve.tensor_tensor(posn[:, :, :], posn[:, :, :], adj[:, :].unsqueeze(2).broadcast_to([P, E, TILES]), ALU.add))
            link(dve.tensor_tensor(posn[:, :, :], posn[:, :, :], by_e(bank[5][:, 0:256].rearrange("p (t e) -> p t e", e=E)), ALU.add))
            for oh, idx in ((oh1, idx1), (oh2, idx2)):
                link(dve.tensor_tensor(tb[:, :, :], oh[:, :, :], posn[:, :, :].rearrange("p e t -> p t e"), ALU.mult))
                link(dve.tensor_reduce(im[:, :], tb[:, :, :], AX.X, ALU.add))
                last = dve.tensor_copy(idx[:, :], im[:, :])
                if idx is idx1:
                    link(last)
            last.then_inc(s["idx_ready"], 1)
            link(dve.tensor_tensor(ended[:, :, :], C["slot"][0:1, :].unsqueeze(2).broadcast_to([1, RT, E]), endp[0:1, :].unsqueeze(1).broadcast_to([1, RT, E]), ALU.is_ge))
            link(dve.tensor_reduce(tile_e[:, :], ended[:, :, :], AX.X, ALU.add))
            link(dve.tensor_scalar(tile_e[:, :], tile_e[:, :], float(E - 1), None, ALU.min))
            link(dve.tensor_scalar(off_b[:, :], tile_e[:, :], float(HC), None, ALU.mult))
            dve.tensor_scalar(off_w[:, :], tile_e[:, :], float(HID), None, ALU.mult).then_inc(s["off_ready"], 1)
            dve.wait_ge(s["ex_ready"], 1)
            link(dve.tensor_scalar(g1[:, :], g2[:, :], 1.0, None, ALU.add))
            link(dve.reciprocal(g1[:, :], g1[:, :]))
            link(dve.tensor_tensor(g2[:, :], g2[:, :], g1[:, :], ALU.mult))
            link(dve.tensor_tensor(gate[:, :, :], oh1[:, :, :], wide(g1), ALU.mult))
            link(dve.tensor_tensor(tb[:, :, :], oh2[:, :, :], wide(g2), ALU.mult))
            link(dve.tensor_tensor(gate[:, :, :], gate[:, :, :], tb[:, :, :], ALU.add))

            def acc(o, i):
                k = 2 * o + i
                x4 = x_all[:, bass.ds(4 * k, 4), :]
                dve.wait_ge(s["proj_ready"], k + 1)
                dve.tensor_tensor(x4, x4, bank[7][:, :].rearrange("p (t d) -> p t d", t=4), ALU.add).then_inc(s["acc_done"], 1)
                dve.wait_ge(s["acc_done"], k + 1)
                dve.tensor_tensor(x4, x4, out_bias[:, :].unsqueeze(1).broadcast_to([P, 4, D]), ALU.add).then_inc(s["bias_done"], 1)

            def gate_out(o, i):
                k = 2 * o + i
                dve.wait_ge(s["g_ready"], k + 1)
                dve.tensor_copy(gate_all[:, bass.ds(512 * k, 512)], bank[4][:, :]).then_inc(s["g_kept"], 1)
                dve.tensor_scalar(xnT[:, bass.ds(512 * k, 512)], bank[4][:, :], 20.0, None, ALU.min).then_inc(s["clamped"], 1)

            dve.wait_ge(s["pre_act"], 1)
            pipeline(dve, 4, 2, [(0, gate_out), (1, acc)])
            dve.wait_ge(s["bias_done"], GROUPS)

            def add_bias(o, i):
                k = 8 * o + i
                e = dve.value_load(off_b[0:1, bass.ds(k, 1)], min_val=0, max_val=(E - 1) * HC)
                dve.wait_ge(s["ht2_ready"], k + 1)
                wait(dve, s["gelu_done"], k - 1)
                c4 = lambda m: m.rearrange("p (c n) -> p c n", c=HC)
                dve.tensor_tensor(c4(hb[:, i % 2, :]), c4(bank[3 + i % 2][:, :]), vec[:, bass.ds(e + R_FC, HC)].unsqueeze(2).broadcast_to([P, HC, P]), ALU.add).then_inc(s["hb_done"], 1)

            def y_out(o, i):
                k = 8 * o + i
                dve.wait_ge(s["y_ready"], k + 1)
                if i % 4 == 0:
                    wait(dve, s[f"st_done{i // 4}"], 16 * o)
                dve.tensor_copy(ys[:, i // 4, i % 4, :], bank[5 + i % 2][:, 0:D]).then_inc(s["ys_done"], 1)

            def mish(o, i):
                if isinstance(o, int) and o == 0:
                    return
                k = o - 1
                n, g, r = xnT[:, bass.ds(512 * k, 512)], gate_all[:, bass.ds(512 * k, 512)], tr[:, 0, :]
                part = tr[:, 0, (i - 2) % 4 * P:((i - 2) % 4 + 1) * P]
                f = (
                    lambda: dve.scalar_tensor_tensor(n, n, 2.0, n, ALU.add, ALU.mult),
                    lambda: dve.tensor_scalar(r, n, 2.0, None, ALU.add),
                    *[lambda: dve.reciprocal(part, part)] * 4,
                    lambda: dve.tensor_tensor(n, n, r, ALU.mult),
                    lambda: dve.tensor_tensor(g, g, n, ALU.mult),
                )[i]
                dve.wait_ge(s["mish_steps"], 8 * k + i + 1)
                f().then_inc(s["mish_steps"], 1)

            dve.wait_ge(s["mish_exp"], 1)
            dve.sem_inc(s["mish_steps"], 1)
            pipeline(dve, RT // 8, 8, [(0, add_bias), (2, y_out), (0, mish)])

            def rope(b, u):
                k = TB * b + u
                dve.wait_ge(s["drained0"], k + 1)
                wait(dve, s["state_ready"], k - 3)
                src = raw[:, u % 4, 0:256].rearrange("p (s h d) -> p s h d", s=2, h=NH)
                dst = qk[:, u % 4, :].rearrange("p (s h d) -> p s h d", s=2, h=NH)
                rt1, rt2 = rt1_r[:, u % 2], rt2_r[:, u % 2]
                wait(dve, s["roped"], k - 1)
                over = lambda m, n: m.unsqueeze(2).broadcast_to([P, 2, NH, n])
                dve.tensor_tensor(rt1[:, :, :, :], src[:, :, :, 0:ROT], over(ropec[:, u, :, :], ROT), ALU.mult)
                dve.tensor_tensor(rt2[:, :, :, 0::2], src[:, :, :, 1:ROT:2], over(ropes[:, u, :, 0::2], ROT // 2), ALU.mult)
                dve.tensor_tensor(rt2[:, :, :, 1::2], src[:, :, :, 0:ROT:2], over(ropes[:, u, :, 1::2], ROT // 2), ALU.mult).then_inc(s["rot_parts"], 1)
                dve.tensor_copy(dst[:, :, :, ROT:HD], src[:, :, :, ROT:HD])
                dve.wait_ge(s["rot_parts"], k + 1)
                dve.tensor_tensor(dst[:, :, :, 0:ROT], rt1[:, :, :, :], rt2[:, :, :, :], ALU.add).then_inc(s["roped"], 1)

            def mask(b, u):
                k = TB * b + u
                dve.wait_ge(s["st_ready"], k + 1)
                wait(dve, s["o_ready"], k - 3)
                dve.tensor_tensor(stm[:, u % 4, :, :], pair[:, :, 0:P],
                                  C["causal"].unsqueeze(1).broadcast_to([P, NH, P]), ALU.mult).then_inc(s["drained2"], 1)

            def ret_out(b, u):
                k = TB * b + u
                dve.wait_ge(s["o_ready"], k + 1)
                dve.tensor_tensor(ret_all[:, k * P:(k + 1) * P], bank[5][:, 0:P], decq[:, u, :], ALU.mult).then_inc(s["drained5"], 1)

            def combine(b, u):
                k = TB * b + u
                dve.wait_ge(s[f"gath{u % 4}"], 32 * (2 * b + u // 4 + 1))
                x1 = x_all[:, bass.ds(k, 1), :].rearrange("p t d -> p (t d)")
                for j, g in enumerate((g1, g2)):
                    dve.scalar_tensor_tensor(x1, yg[:, u % 4, j, :], g[:, bass.ds(k, 1)], x1, ALU.mult, ALU.add).then_inc(s["part_sums" if j == 0 else "combined"], 1)
                    if j == 0:
                        dve.wait_ge(s["part_sums"], k + 1)

            def norm_mean(b):
                dve.wait_ge(s["gtot_ready"], b + 1)
                dve.tensor_scalar(gnm[:, b:b + 1], bank[7][:, 0:1], -1.0 / (S * HD), None, ALU.mult).then_inc(s["gmean_ready"], 1)
                dve.wait_ge(s["gmean_ready"], b + 1)
                dve.sem_inc(s["drained7"], 1)

            def norm_var(b):
                dve.wait_ge(s["gtot2_ready"], b + 1)
                dve.tensor_scalar(gva[:, b:b + 1], bank[7][:, 0:1], 1.0 / (S * HD), EPS, ALU.mult, ALU.add).then_inc(s["gve_ready"], 1)
                dve.wait_ge(s["gve_ready"], b + 1)
                dve.sem_inc(s["drained7"], 1)

            def norm_scale(b):
                dve.wait_ge(s["gr_ready"], b + 1)
                dve.tensor_tensor(gna[:, b:b + 1], gvb[:, b:b + 1], gn[:, 0:1], ALU.mult).then_inc(s["gna_ready"], 1)
                dve.wait_ge(s["gna_ready"], b + 1)
                dve.scalar_tensor_tensor(gnc[:, b:b + 1], gnm[:, b:b + 1], gna[:, b:b + 1], gn[:, 1:2], ALU.mult, ALU.add).then_inc(s["gac_ready"], 1)

            def y_mul(k):
                dve.wait_ge(s["yn_done"], k + 1)
                wait(dve, s["wo_ready"], k - 1)
                dve.tensor_tensor(yT[:, k % 2, :], yn_r[:, k % 2, :], gate_all[:, k * 512:(k + 1) * 512], ALU.mult).then_inc(s["yt_done"], 1)

            def y2(k):
                y4 = y2_all[:, 4 * k:4 * k + 4, :]
                dve.wait_ge(s["wo_ready"], k + 1)
                dve.tensor_tensor(y4, bank[6][:, :].rearrange("p (t d) -> p t d", t=4), xn_all[:, 4 * k:4 * k + 4, :], ALU.add).then_inc(s["drained6"], 1)
                dve.wait_ge(s["drained6"], 2 * k + 1)
                moments(lambda v: y2_all[:, 4 * k + v, :], k % 2, k, "st2", "ag2", "ve2_ready")

            def z0(k):
                dve.wait_ge(s["r2_ready"], k + 1)
                for v in range(4):
                    last = dve.tensor_scalar(xr[:, k % 2, v, :], y2_all[:, 4 * k + v, :], mv[:, k % 2, v, 0:1], ra[:, k % 2, v:v + 1], ALU.subtract, ALU.mult)
                last.then_inc(s["z0_done"], 1)
                x4 = x_all[:, 4 * k:4 * k + 4, :]
                dve.tensor_tensor(x4, x4, y2_all[:, 4 * k:4 * k + 4, :], ALU.add).then_inc(s["xy_done"], 1)

            def final(k):
                dve.wait_ge(s["m2_ready"], k + 1)
                wait(dve, s[f"out_done{k % 2}"], 16 * (k // 2))
                dve.wait_ge(s["xy_done"], k + 1)
                dve.tensor_tensor(ob[:, k % 2, :, :], bank[7][:, :].rearrange("p (t d) -> p t d", t=4), x_all[:, 4 * k:4 * k + 4, :], ALU.add).then_inc(s["fin_ready"], 1)
                dve.wait_ge(s["fin_ready"], k + 1)
                dve.sem_inc(s["drained7"], 1)

            dve.wait_ge(s["tables_in"], 16)
            pipeline(dve, B, TB, [(0, rope), (3, mask), (4, ret_out), (2, combine), (5, by_sequence(norm_mean)), (7, by_sequence(norm_var)), (8, by_sequence(norm_scale)),
                                  (13, by_group(y_mul)), (14, by_group(y2)), (15, by_group(z0)), (18, by_group(final))])


_INS = ["L0_attn_x", "L0_attn_ln1_w", "L0_attn_ln1_b", "L0_attn_wqkv_w", "L0_attn_wg_w", "L0_attn_wo_w", "L0_attn_gn_w", "L0_attn_gn_b",
        "L0_attn_ln2_w", "L0_attn_ln2_b", "L0_attn_w1_w", "L0_attn_w1_b", "L0_attn_w2_w", "L0_attn_w2_b", "L0_ffn_Wfc_s", "L0_ffn_bfc_s",
        "L0_ffn_Wproj_s", "L0_ffn_bproj_s", "L0_ffn_Wr", "L0_ffn_Wfc", "L0_ffn_bfc", "L0_ffn_Wproj", "L0_ffn_bproj"]


def kernel(**inputs):
    import concourse.bacc as bacc
    from concourse.bass_utils import run_bass_kernel_spmd

    nc = bacc.Bacc("TRN2", target_bir_lowering=False, num_devices=1)
    arrays, args = {}, {}
    for name in _INS:
        arrays[name] = np.ascontiguousarray(inputs[name])
        args[name] = nc.dram_tensor(name, arrays[name].shape, F32, kind="ExternalInput").ap()
    parts, cols, at = constants(), {}, 0
    for name, v in parts.items():
        cols[name] = (at, at + v.shape[1])
        at += v.shape[1]
    arrays["const"] = np.ascontiguousarray(np.concatenate(list(parts.values()), axis=1).astype(np.float32))
    const = nc.dram_tensor("const", arrays["const"].shape, F32, kind="ExternalInput").ap()
    out = nc.dram_tensor("out", (B, S, D), F32, kind="ExternalOutput").ap()
    build(nc, args, const, cols, out)
    return run_bass_kernel_spmd(nc, [arrays], core_ids=[0]).results[0]["out"]
```

```python
from contextlib import ExitStack

import numpy as np

import concourse.bass as bass
from concourse import mybir

ALU = mybir.AluOpType
ACT = mybir.ActivationFunctionType
AX = mybir.AxisListType
F32 = mybir.dt.float32
F16 = mybir.dt.float16
I32 = mybir.dt.int32

P = 128
B, S, D = 4, 1024, 128
TILES = B * S // P
GROUPS = TILES // 4
TB = S // P
NH, HD, ROT = 2, 64, 32
E, HID = 8, 512
HC = HID // P
EPS = 1e-5
SW = 2 * P
RT = 2 * B * S // SW + E
BLOCKS = RT // 2
XS = 4096.0
TOP = 14


def constants():
    f4 = np.float32
    half = np.arange(0, ROT, 2, dtype=f4)
    inv_freq = (f4(1.0) / np.power(f4(10000.0), half / f4(ROT))).astype(f4)
    t = np.arange(S, dtype=f4)
    freqs = np.repeat((t[:, None] * inv_freq).astype(f4), 2, axis=-1).astype(np.float64)
    base = ((half + 0.4 * ROT) / (1.4 * ROT)).astype(np.float64)
    scale = base[None, :] ** ((t.astype(np.float64) - S // 2) / 512.0)[:, None]
    scale = np.concatenate((scale, scale), axis=-1)
    sign = np.where(np.arange(ROT) % 2 == 0, -1.0, 1.0)
    cos, sin = np.cos(freqs), np.sin(freqs) * sign
    both = lambda a: np.stack([a * scale, a / scale], 1)
    tiled = lambda a: a.reshape(TB, P, -1).transpose(1, 0, 2).reshape(P, -1)
    gamma = 1.0 - 2.0 ** (-5.0 - np.arange(NH))
    pos = np.arange(S, dtype=np.float64)[:, None]
    row = np.arange(P)
    full = lambda v: np.broadcast_to(np.asarray(v, np.float64), (P, len(v)))
    return {
        "ident": np.eye(P),
        "before": (row[:, None] < row[None, :]) * 1.0,
        "causal": (row[:, None] <= row[None, :]) * 1.0,
        "ones": np.ones((P, 256)),
        "heads": (row[:, None] == row[None, :] // HD) * 1.0,
        "head": (row[:, None] // HD == row[None, :] // HD) * 1.0,
        "mhalf": np.full((P, TILES), -0.5),
        "eps": np.full((P, TILES), EPS),
        "em8": full(np.arange(E) - E),
        "slot": full(np.arange(RT) * SW),
        "ropec": tiled(both(cos)),
        "ropes": tiled(both(sin)),
        "deck": tiled(gamma[None, :] ** -pos),
        "decq": np.repeat(gamma[None, :] ** pos, HD, axis=1).T,
    }


def pipeline(eng, outer, inner, stages):
    longest = max(lag for lag, _ in stages)
    filled = (longest + 1) // inner + 1
    def step(o, i):
        for lag, fn in stages:
            oo, ii = o + (i - lag) // inner, (i - lag) % inner
            if not isinstance(oo, int) or 0 <= oo < outer:
                fn(oo, ii)

    for o in range(filled):
        for i in range(inner):
            step(o, i)
    if outer - filled == 1:
        filled, o = outer, outer - 1
        for i in range(inner):
            step(o, i)
    if filled < outer:
        with eng.Fori(filled, outer) as o:
            for i in range(inner):
                step(o, i)
    for i in range(longest):
        step(outer, i)


def written_out(outer, inner, stages):
    for step in range(outer * inner + max(lag for lag, _ in stages)):
        for lag, fn in stages:
            if 0 <= step - lag < outer * inner:
                fn((step - lag) // inner, (step - lag) % inner)


LAG = dict(sum1=8, mean=9, sum2=11, var=11, rsqrt=10, scale=12, yn=13, y_mul=13, wo=15, y2=16, second=17, z0=19,
           zt=20, z=20, w1=24, gelu=24, w2=27, final=28)


def groups(stages):
    written_out(1, GROUPS, [(lag, lambda o, i, fn=fn: fn(i)) for lag, fn in stages])


def by_group(fn):
    return lambda b, u: fn(2 * b + u - (TB - 2)) if u >= TB - 2 else None


def by_sequence(fn):
    return lambda b, u: fn(b) if u == TB - 1 else None


def wait(eng, sem, n):
    if not isinstance(n, int) or n > 0:
        eng.wait_ge(sem, n)


def build(nc, a, const, cols, out):
    with ExitStack() as ctx:
        def sb(name, shape, dt=F32):
            return ctx.enter_context(nc.sbuf_tensor(name, shape, dt))

        def sem(name):
            return ctx.enter_context(nc.semaphore(name))

        bank = [ctx.enter_context(nc.psum_tensor(f"bank{i}", [P, 512], F32)) for i in range(2)]
        pairs = [ctx.enter_context(nc.psum_tensor(f"bank{n}_{n + 1}", [P, 2, 512], F32)) for n in (2, 4)]
        pair = pairs[0]
        bank += [m[:, j, :] for m in pairs for j in range(2)]
        bank += [ctx.enter_context(nc.psum_tensor(f"bank{i}", [P, 512], F32)) for i in range(6, 8)]

        slots_x = nc.dram_tensor("slots_x", (RT * SW, D), F32, kind="Internal").ap()
        slots_y = nc.dram_tensor("slots_y", (RT * SW, D), F32, kind="Internal").ap()

        cst = sb("cst", [P, const.shape[1]])
        C = {k: cst[:, lo:hi] for k, (lo, hi) in cols.items()}
        ident, ones = C["ident"], C["ones"]
        ropec = C["ropec"].rearrange("p (t s d) -> p t s d", t=TB, s=2)
        ropes = C["ropes"].rearrange("p (t s d) -> p t s d", t=TB, s=2)
        decq = C["decq"].rearrange("p (t n) -> p t n", t=TB)
        deck = C["deck"].rearrange("p (t h) -> p t h", t=TB)
        w_in = sb("w_in", [P, 384])
        wg = sb("wg", [P, D])
        wo, w1, w2 = sb("wo", [P, D]), sb("w1", [P, D]), sb("w2", [P, D])
        wr = sb("wr", [P, E])
        wfc_s, wproj_s = sb("wfc_s", [P, HID]), sb("wproj_s", [P, HC, D])
        wfc, wproj = sb("wfc", [P, E * HID]), sb("wproj", [P, E * HC * D])
        bproj = sb("bproj", [P, E * D])
        wfc16 = wfc[:, :].bitcast(F16).rearrange("p (s n) -> p s n", s=2)
        amax, scale, inverse = sb("amax", [P, 1]), sb("scale", [P, 1]), sb("inverse", [P, 1])
        amax_row, exponent = sb("amax_row", [1, 1]), sb("exponent", [P, 1], I32)
        bias16 = sb("bias16", [P, E * HC])
        gelu_scale = sb("gelu_scale", [P, 1])
        rows = sb("rows", [48, P])
        vec = sb("vec", [P, 48])
        out_rows = sb("out_rows", [2, D])
        out_bias = sb("out_bias", [P, D])
        gn_rows = sb("gn_rows", [NH, 2])
        gn = sb("gn", [P, 2])
        R_FC, R_FCS, R_L1W, R_L1B, R_L2W, R_L2B, R_W1B = 0, 32, 36, 37, 38, 39, 40
        N_ROWS = 41

        x_all = sb("x_all", [P, TILES, D])
        xn_all = sb("xn_all", [P, TILES, D])
        xnT = sb("xnT", [P, TILES * P])
        hT = sb("hT", [P, TILES * P])
        gate_all = sb("gate_all", [P, TILES * P])
        y2_all = gate_all[:, :].rearrange("p (t d) -> p t d", d=D)
        ret_all = sb("ret_all", [P, TILES * P])

        stats = sb("stats", [P, GROUPS, 4, 6])
        mv = sb("mv", [P, GROUPS, 4, 2])
        ve = sb("ve", [P, GROUPS, 4])
        negm = sb("negm", [P, 2, 4])
        ra, rb, rc = (sb(n, [P, GROUPS, 4]) for n in ("ra", "rb", "rc"))
        xr, hr = sb("xr", [P, 2, 4, D]), sb("hr", [P, 2, 4, D])
        tr = sb("tr", [P, 2, 512])
        work = sb("work", [P, 4096])
        wfc32 = ret_all[:, :]
        gs = work[:, :].rearrange("p (r c n) -> p r c n", r=2, c=HC)
        xin = work[:, 0:1024].rearrange("p (r u n) -> p r u n", r=2, u=4)
        hb = [work[:, j * 1024:(j + 1) * 1024] for j in range(1, 4)]
        hb.append(hr[:, :, :, :].rearrange("p r u n -> p (r u n)"))
        x16 = xr[:, :, :, :].rearrange("p r u n -> p (r u n)").bitcast(F16).rearrange("p (s r n) -> p s r n", s=2, r=2)
        xh, xl = x16[:, 0], x16[:, 1]
        ys = sb("ys", [P, 2, 4, D])
        zeros = sb("zeros", [P, 256])
        raw = work[:, 0:512].rearrange("p (r s h d) -> p r s h d", r=4, s=2, h=NH)
        qk = work[:, 1024:3072].rearrange("p (r n) -> p r n", r=8)
        rt1_r, rt2_r = sb("rt1", [P, 2, 2, NH, ROT]), sb("rt2", [P, 2, 2, NH, ROT])
        qkT = [m[:, j * 256:(j + 1) * 256] for m in (work[:, 3072:4096], tr[:, :, :].rearrange("p r n -> p (r n)")) for j in range(4)]
        vd = hr[:, :, :, :].rearrange("p r u n -> p (r u) n")
        stm = wproj[:, 3072:4096].rearrange("p (r h n) -> p r h n", r=4, h=NH)
        rs = sb("rs", [P, 4, D])
        yg = sb("yg", [P, 4, 2, D])
        ob = wfc[:, 3072:4096].rearrange("p (r u n) -> p r u n", r=2, u=4)
        oh1, oh2 = sb("oh1", [P, TILES, E]), sb("oh2", [P, TILES, E])
        spare = ret_all[:, :]
        ta, tb = (spare[:, j * 256:(j + 1) * 256].rearrange("p (t e) -> p t e", e=E) for j in range(2))
        m1, m2, im = sb("m1", [P, TILES]), sb("m2", [P, TILES]), sb("im", [P, TILES])
        dd, g1, g2 = sb("dd", [P, TILES]), sb("g1", [P, TILES]), sb("g2", [P, TILES])
        tot, cum, posn = (spare[:, j * 256:(j + 1) * 256].rearrange("p (e t) -> p e t", e=E) for j in range(2, 5))
        cnt, pad, endp, adj = (sb(n, [P, E]) for n in ("cnt", "pad", "endp", "adj"))
        cnti = sb("cnti", [P, E], I32)
        idx1, idx2 = sb("idx1", [P, TILES], I32), sb("idx2", [P, TILES], I32)
        ended = ret_all[0:1, 1280:1280 + RT * E].rearrange("p (j e) -> p j e", e=E)
        tile_e = sb("tile_e", [1, RT])
        off_w, off_b, off_y = (sb(n, [1, RT], I32) for n in ("off_w", "off_b", "off_y"))
        gst, gmv = sb("gst", [P, B, 2, 6]), sb("gmv", [P, B, 2])
        gdev, gsq, gnm, gva, gvb, gna, gnc = (sb(n, [P, B]) for n in ("gdev", "gsq", "gnm", "gva", "gvb", "gna", "gnc"))
        yn_r = wproj[:, 2048:3072].rearrange("p (r n) -> p r n", r=2)
        yT, zT, aT = (wfc[:, j * 1024:(j + 1) * 1024].rearrange("p (r n) -> p r n", r=2) for j in range(3))

        names = """x_in2 x_in3 x_in4 x_in5 x_in6 x_in7 tables_in cst_in vec_in win_in wr_in wshared_in wexp_in watt_in zero_in x_in0 x_in1
            zeroed pre_pe pre_act ve_ready r_ready xn_done tr_ready xnt_done ht_done lg_ready link_v link_p mask_ready rank_ready
            dd_ready ex_ready idx_ready off_ready scattered fc_ready gs_done proj_ready acc_done xs_in0 xs_in1 xt_ready h_ready
            hb_done gelu_done y_ready ys_done st_done0 st_done1 roped qkt_ready st_ready state_ready o_ready gath0 gath1 gath2
            gath3 combined gsum_ready gtot_ready gmean_ready gsq_ready gtot2_ready gve_ready gr_ready gac_ready mish_exp sp_passed
            st1 ag1 st2 ag2 bias_done rot_parts part_sums xy_done yn_done wo_ready ve2_ready r2_ready z0_done t2_ready m1_ready
            m2_ready fin_ready out_done0 out_done1 clamped const drained0 drained1 drained2 drained4 drained5 drained6 drained7
            g_kept g_ready gna_ready mish_steps negm_ready pow2 gst_done trh_ready r2n_ready h0_done raw_done temps_free
            amax_ready amaxt_ready arow_ready abc_ready scale_ready high_done low_done split_done xh_done xl_done qkv_ready
            rs_zero yt_done""".split()
        s = {n: sem(n) for n in names}
        block = ctx.enter_context(nc.Block())

        x_d = a["L0_attn_x"].rearrange("b (t p) d -> p (b t) d", p=P)
        out_d = out.rearrange("b (t p) d -> p (b t) d", p=P)
        one_row = lambda v: v.rearrange("(o n) -> o n", o=1)

        @block.sync
        def _(sp):
            def sp_wait(sem, n):
                wait(sp, sem, n)
                if not isinstance(n, int):
                    sp.sem_inc(s["sp_passed"], 1)

            def load_x(k):
                sp.dma_start(x_all[:, 4 * k:4 * k + 4, :], x_d[:, 4 * k:4 * k + 4, :]).then_inc(s[f"x_in{k}"], 16)

            load_x(0)
            late = cols["ropec"][0]
            sp.dma_start(cst[:, 0:late], const[:, 0:late]).then_inc(s["cst_in"], 16)
            load_x(1)
            sp.dma_start(wr[:, :], a["L0_ffn_Wr"]).then_inc(s["wr_in"], 16)
            for k in range(2, GROUPS):
                load_x(k)
            for i, v in enumerate((a["L0_attn_ln1_w"], a["L0_attn_ln1_b"], a["L0_attn_ln2_w"], a["L0_attn_ln2_b"], a["L0_attn_w1_b"])):
                sp.dma_start(rows[R_L1W + i:R_L1W + i + 1, :], one_row(v)).then_inc(s["vec_in"], 16)
            sp.dma_start(rows[R_FC:R_FC + E * HC, :], a["L0_ffn_bfc"].rearrange("e (c p) -> (e c) p", p=P)).then_inc(s["vec_in"], 16)
            sp.dma_start(rows[R_FCS:R_FCS + HC, :], a["L0_ffn_bfc_s"].rearrange("(c p) -> c p", p=P)).then_inc(s["vec_in"], 16)
            sp.dma_start(out_rows[0:1, :], one_row(a["L0_attn_w2_b"])).then_inc(s["vec_in"], 16)
            sp.dma_start(out_rows[1:2, :], one_row(a["L0_ffn_bproj_s"])).then_inc(s["vec_in"], 16)
            sp.dma_start(gn_rows[:, 0:1], a["L0_attn_gn_w"].rearrange("(n o) -> n o", o=1)).then_inc(s["vec_in"], 16)
            sp.dma_start(gn_rows[:, 1:2], a["L0_attn_gn_b"].rearrange("(n o) -> n o", o=1)).then_inc(s["vec_in"], 16)
            sp.dma_start(wfc_s[:, :], a["L0_ffn_Wfc_s"]).then_inc(s["wshared_in"], 16)
            sp.dma_start(wproj_s[:, :, :], a["L0_ffn_Wproj_s"].rearrange("(c p) d -> p c d", p=P)).then_inc(s["wshared_in"], 16)
            sp.dma_start(wg[:, :], a["L0_attn_wg_w"]).then_inc(s["wshared_in"], 16)
            sp.wait_ge(s["zero_in"], 1)
            sp.dma_start(slots_x.rearrange("(p q n) d -> p q (n d)", p=P, n=2), zeros[:, :].unsqueeze(1).broadcast_to([P, RT * SW // P // 2, 256])).then_inc(s["zeroed"], 16)
            sp.dma_start(wproj[:, :].rearrange("p (e c d) -> p e c d", e=E, c=HC), a["L0_ffn_Wproj"].rearrange("e (c p) d -> p e c d", p=P)).then_inc(s["watt_in"], 16)
            sp.wait_ge(s["temps_free"], 1)
            sp.dma_start(wfc32.rearrange("p (e n) -> p e n", e=E), a["L0_ffn_Wfc"].rearrange("e p n -> p e n")).then_inc(s["wexp_in"], 16)
            sp.dma_start(bproj[:, :], one_row(a["L0_ffn_bproj"].rearrange("e d -> (e d)")).broadcast_to([P, E * D])).then_inc(s["watt_in"], 16)
            for h in range(NH):
                sp.dma_start(w_in[:, :].rearrange("p (s h d) -> p s h d", s=3, h=NH)[:, :, h, :],
                             a["L0_attn_wqkv_w"].rearrange("p (h s d) -> p s h d", h=NH, s=3)[:, :, h, :]).then_inc(s["win_in"], 16)
            sp.dma_start(cst[:, late:], const[:, late:]).then_inc(s["tables_in"], 16)
            for w, v in ((wo, "wo"), (w1, "w1"), (w2, "w2")):
                sp.dma_start(w[:, :], a[f"L0_attn_{v}_w"]).then_inc(s["watt_in"], 16)

            def load_slots(o, i):
                read, n, q = 2 * o + i - 1, 16 * o, 2 * o + i
                sp_wait(s["xt_ready"], read)
                sp_wait(s[f"xs_in{i}"], n)
                sp.dma_start(xin[:, i, :, :], slots_x.rearrange("(q u p) d -> q p u d", u=4, p=P)[bass.ds(q, 1)].rearrange("q p u d -> p (q u) d")).then_inc(s[f"xs_in{i}"], 16)

            def store_slots(o, i):
                done, n, q = 4 * o + 2 * i + 2, 16 * o, 2 * o + i
                sp_wait(s["ys_done"], done)
                sp_wait(s[f"st_done{i}"], n)
                sp.dma_start(slots_y.rearrange("(q u p) d -> q p u d", u=4, p=P)[bass.ds(q, 1)].rearrange("q p u d -> p (q u) d"), ys[:, i, :, :]).then_inc(s[f"st_done{i}"], 16)

            sp.wait_ge(s["scattered"], 16 * 2 * TILES)
            sp.wait_ge(s["proj_ready"], GROUPS)
            pipeline(sp, BLOCKS // 2, 2, [(0, load_slots), (3, store_slots)])

            def store_out(o, i):
                done, n, t = 2 * o + i + 1, 16 * o, 8 * o + 4 * i
                sp_wait(s["fin_ready"], done)
                sp_wait(s[f"out_done{i}"], n)
                sp.dma_start(out_d[:, bass.ds(t, 4), :], ob[:, i, :, :]).then_inc(s[f"out_done{i}"], 16)

            pipeline(sp, B, 2, [(0, store_out)])
            sp.wait_ge(s["out_done0"], 16 * B)
            sp.wait_ge(s["out_done1"], 16 * B)

        @block.tensor
        def _(pe):
            pe.wait_ge(s["cst_in"], 16)

            def p1_transpose(k):
                i = k % 2
                pe.wait_ge(s["xn_done"], k + 1)
                wait(pe, s["xnt_done"], k - 1)
                for u in range(4):
                    last = pe.transpose(bank[i][:, u * P:(u + 1) * P], xn_all[:, 4 * k + u, :], ident)
                last.then_inc(s["tr_ready"], 1)

            def p1_transpose_h(k):
                pe.wait_ge(s["h0_done"], k + 1)
                wait(pe, s["ht_done"], k)
                for u in range(4):
                    last = pe.transpose(bank[5][:, u * P:(u + 1) * P], hr[:, k % 2, u, :], ident)
                last.then_inc(s["trh_ready"], 1)

            def p1_logits(k):
                pe.wait_ge(s["xnt_done"], k + 1)
                if k == 0:
                    pe.wait_ge(s["wr_in"], 16)
                for u in range(4):
                    at = 4 * k + u
                    last = pe.matmul(bank[4][:, at * E:(at + 1) * E], xnT[:, at * P:(at + 1) * P], wr[:, :], start=True, stop=True)
                last.then_inc(s["lg_ready"], 1)

            groups([(0, p1_transpose), (1, p1_logits)])

            pe.wait_ge(s["vec_in"], 16 * 11)
            pe.transpose(bank[5][:, 0:N_ROWS], rows[0:N_ROWS, :], ident[0:N_ROWS, 0:N_ROWS])
            pe.matmul(bank[6][:, 0:D], ones[0:2, 0:P], out_rows[:, :], start=True, stop=True)
            pe.matmul(bank[6][:, D:D + 2], C["heads"][0:NH, :], gn_rows[:, :], start=True, stop=True).then_inc(s["pre_pe"], 1)

            def ranks():
                pe.wait_ge(s["mask_ready"], 1)
                pe.wait_ge(s["pre_act"], 1)
                pe.matmul(bank[6][:, 256:512], C["before"], ta[:, :, :].rearrange("p t e -> p (t e)"), start=True, stop=True)
                pe.matmul(bank[6][:, 0:256], ones[:, 0:P], ta[:, :, :].rearrange("p t e -> p (t e)"), start=True, stop=True).then_inc(s["rank_ready"], 1)

            def fc(k):
                for c in range(HC):
                    wait(pe, s["gs_done"], HC * (k - 1) + c + 1)
                    pe.matmul(bank[c][:, :], wfc_s[:, c * P:(c + 1) * P], xnT[:, k * 512:(k + 1) * 512], start=True, stop=True).then_inc(s["fc_ready"], 1)

            def gate_mm(k):
                pe.wait_ge(s["ht_done"], k + 1)
                wait(pe, s["clamped"], k)
                pe.matmul(bank[4][:, :], wg[:, :], hT[:, k * 512:(k + 1) * 512], start=True, stop=True).then_inc(s["g_ready"], 1)

            def proj(k):
                pe.wait_ge(s["gs_done"], HC * (k + 1))
                wait(pe, s["acc_done"], k)
                for u in range(4):
                    for c in range(HC):
                        last = pe.matmul(bank[7][:, u * P:(u + 1) * P], gs[:, k % 2, c, u * P:(u + 1) * P], wproj_s[:, c, :], start=(c == 0), stop=(c == HC - 1))
                last.then_inc(s["proj_ready"], 1)

            def largest(k):
                if k == 1:
                    pe.wait_ge(s["amax_ready"], 1)
                    pe.transpose(bank[6][0:1, 0:P], amax[:, :], ident).then_inc(s["amaxt_ready"], 1)
                if k == 2:
                    pe.wait_ge(s["arow_ready"], 1)
                    pe.matmul(bank[6][:, 0:1], ones[0:1, 0:P], amax_row[:, :], start=True, stop=True).then_inc(s["abc_ready"], 1)

            ranks()
            pe.wait_ge(s["wshared_in"], 48)
            groups([(0, fc), (0, p1_transpose_h), (1, gate_mm), (1, proj), (1, largest)])

            pe.wait_ge(s["off_ready"], 1)
            pe.wait_ge(s["split_done"], 1)
            pe.wait_ge(s["watt_in"], 16 * 5)
            pe.wait_ge(s["acc_done"], GROUPS)

            def expert(o, i):
                return pe.value_load(off_w[0:1, bass.ds(4 * o + i, 1)], min_val=0, max_val=(E - 1) * HID)

            def x_transpose(o, i):
                if i % 2 == 0:
                    pe.wait_ge(s[f"xs_in{i // 2}"], 16 * (o + 1))
                    wait(pe, s["xl_done"], 2 * o + i // 2 - 1)
                    for v in range(4):
                        last = pe.transpose(bank[i // 2][:, v * P:(v + 1) * P], xin[:, i // 2, v, :], ident)
                    last.then_inc(s["xt_ready"], 1)

            def up(o, i):
                e = expert(o, i)
                if i % 2 == 0:
                    pe.wait_ge(s["xl_done"], 2 * o + i // 2 + 1)
                wait(pe, s["hb_done"], 4 * o + i - 1)
                for c in range(HC):
                    to = pairs[i % 2][:, :, :].rearrange("p b n -> p (b n)")[:, c * SW:(c + 1) * SW]
                    for j, (w, x) in enumerate(((0, xh), (0, xl), (1, xh))):
                        last = pe.matmul(to, wfc16[:, w, bass.ds(e + c * P, P)], x[:, i // 2, i % 2 * SW:(i % 2 + 1) * SW], start=(j == 0), stop=(j == 2))
                last.then_inc(s["h_ready"], 1)

            def down(o, i):
                k = 4 * o + i
                e = expert(o, i)
                pe.wait_ge(s["gelu_done"], k + 1)
                wait(pe, s["ys_done"], k - 1)
                for v in range(2):
                    for c in range(HC):
                        last = pe.matmul(bank[6 + i % 2][:, v * P:(v + 1) * P], hb[i % 4][:, c * SW + v * P:c * SW + (v + 1) * P], wproj[:, bass.ds(e + c * D, D)],
                                         start=(c == 0), stop=(c == HC - 1))
                last.then_inc(s["y_ready"], 1)

            pipeline(pe, RT // 4, 4, [(0, x_transpose), (2, up), (3, down)])

            pe.wait_ge(s["win_in"], 32)
            pe.wait_ge(s["watt_in"], 16 * 5)
            pe.wait_ge(s["rs_zero"], 1)
            used = dict.fromkeys(range(8), 0)

            def take(n):
                if n >= 6 and used[n] == 0:
                    pe.wait_ge(s["ys_done"], RT)
                wait(pe, s[f"drained{n}"], used[n])
                used[n] += 1

            def project(b, u):
                k = TB * b + u
                take(0)
                pe.matmul(bank[0][:, 0:384], hT[:, k * P:(k + 1) * P], w_in[:, :], start=True, stop=True).then_inc(s["qkv_ready"], 1)

            def qk_transpose(b, u):
                k = TB * b + u
                pe.wait_ge(s["roped"], k + 1)
                take(1)
                for j in range(2):
                    last = pe.transpose(bank[1][:, j * P:(j + 1) * P], qk[:, u % 8, j * P:(j + 1) * P], ident)
                last.then_inc(s["qkt_ready"], 1)

            def scores(b, u):
                k = TB * b + u
                pe.wait_ge(s["drained1"], k + 1)
                take(2)
                for h in range(NH):
                    hp = slice(h * HD, (h + 1) * HD)
                    last = pe.matmul(pair[:, h, 0:P], qkT[u][hp, P:2 * P], qkT[u][hp, 0:P], start=True, stop=True)
                last.then_inc(s["st_ready"], 1)
                pe.wait_ge(s["drained0"], k + 1)
                take(4)
                pe.matmul(bank[4][:, 0:D], qk[:, u % 8, P:2 * P], vd[:, u % 8, :], start=(u == 0), stop=True, skip_group_check=True).then_inc(s["state_ready"], 1)

            def outputs(b, u):
                k = TB * b + u
                pe.wait_ge(s["drained2"], k + 1)
                wait(pe, s["drained4"], k)
                take(5)
                if u > 0:
                    pe.matmul(bank[5][:, 0:P], rs[:, (u - 1) % 4, :], qkT[u][:, 0:P], start=True, stop=False, skip_group_check=True)
                for h in range(NH):
                    hp = slice(h * HD, (h + 1) * HD)
                    last = pe.matmul(bank[5][hp, 0:P], vd[:, u % 8, hp], stm[:, u % 4, h, :], start=(u == 0), stop=True, skip_group_check=True)
                last.then_inc(s["o_ready"], 1)

            def norm_sum(b, src, ready, done):
                pe.wait_ge(s[ready], b + 1)
                take(6)
                pe.matmul(bank[6][:, 0:1], C["head"], src, start=True, stop=True).then_inc(s[done], 1)

            def wo_mm(k):
                pe.wait_ge(s["yt_done"], k + 1)
                take(6)
                for v in range(4):
                    last = pe.matmul(bank[6][:, v * P:(v + 1) * P], yT[:, k % 2, v * P:(v + 1) * P], wo[:, :], start=True, stop=True)
                last.then_inc(s["wo_ready"], 1)

            def z_transpose(k):
                pe.wait_ge(s["z0_done"], k + 1)
                take(6)
                for v in range(4):
                    last = pe.transpose(bank[6][:, v * P:(v + 1) * P], xr[:, k % 2, v, :], ident)
                last.then_inc(s["t2_ready"], 1)

            def w1_mm(k):
                pe.wait_ge(s["drained6"], 6 * (k // 2) + 5 + k % 2)
                take(7)
                pe.matmul(bank[7][:, :], w1[:, :], zT[:, k % 2, :], start=True, stop=True).then_inc(s["m1_ready"], 1)

            def w2_mm(k):
                take(7)
                for v in range(4):
                    last = pe.matmul(bank[7][:, v * P:(v + 1) * P], aT[:, k % 2, v * P:(v + 1) * P], w2[:, :], start=True, stop=True)
                last.then_inc(s["m2_ready"], 1)

            written_out(B, TB, [(0, project), (2, qk_transpose), (5, outputs), (3, scores),
                                (LAG["sum1"], by_sequence(lambda b: norm_sum(b, gmv[:, b, 0:1], "gsum_ready", "gtot_ready"))),
                                (LAG["sum2"], by_sequence(lambda b: norm_sum(b, gsq[:, b:b + 1], "gsq_ready", "gtot2_ready"))),
                                (LAG["wo"], by_group(wo_mm)), (LAG["zt"], by_group(z_transpose)), (LAG["w1"], by_group(w1_mm)), (LAG["w2"], by_group(w2_mm))])

        @block.scalar
        def _(act):
            def p1_copy(k):
                act.wait_ge(s["tr_ready"], k + 1)
                act.activation(xnT[:, k * 512:(k + 1) * 512], bank[k % 2][:, :], ACT.Copy).then_inc(s["xnt_done"], 1)

            def p1_copy_h(k):
                act.wait_ge(s["trh_ready"], k + 1)
                act.activation(hT[:, k * 512:(k + 1) * 512], bank[5][:, :], ACT.Identity, bias=vec[:, R_L1B:R_L1B + 1], scale=vec[:, R_L1W:R_L1W + 1]).then_inc(s["ht_done"], 1)

            def p1_second(k):
                act.wait_ge(s["xn_done"], k + 1)
                act.wait_ge(s["r2n_ready"], 1)
                wait(act, s["trh_ready"], k - 1)
                for u in range(4):
                    last = act.activation(hr[:, k % 2, u, :], xn_all[:, 4 * k + u, :], ACT.Identity, scale=rb[:, k, u:u + 1])
                last.then_inc(s["h0_done"], 1)

            groups([(0, p1_copy)])
            act.wait_ge(s["pre_pe"], 1)
            act.activation(vec[:, 0:N_ROWS], bank[5][:, 0:N_ROWS], ACT.Copy)
            act.activation(out_bias[:, :], bank[6][:, 0:D], ACT.Copy)
            act.activation(gn[:, :], bank[6][:, D:D + 2], ACT.Copy).then_inc(s["pre_act"], 1)
            act.wait_ge(s["pre_act"], 1)
            act.wait_ge(s["dd_ready"], 1)
            act.activation(g2[:, :], dd[:, :], ACT.Exp).then_inc(s["ex_ready"], 1)

            def shared_gelu(k):
                wait(act, s["proj_ready"], k - 1)
                for c in range(HC):
                    act.wait_ge(s["fc_ready"], HC * k + c + 1)
                    act.activation(gs[:, k % 2, c, :], bank[c][:, :], ACT.Gelu_apprx_tanh, bias=vec[:, R_FCS + c:R_FCS + c + 1]).then_inc(s["gs_done"], 1)

            def high_part(k):
                if k >= 4:
                    part = slice((k - 4) * 1024, (k - 3) * 1024)
                    act.wait_ge(s["scale_ready"], 1)
                    act.activation(wfc16[:, 0, part], wfc32[:, part], ACT.Identity, scale=scale[:, 0:1]).then_inc(s["high_done"], 1)

            groups([(0, p1_second), (0, shared_gelu), (0, p1_copy_h), (0, high_part)])
            act.wait_ge(s["clamped"], GROUPS)
            act.activation(xnT[:, :], xnT[:, :], ACT.Exp).then_inc(s["mish_exp"], 1)
            act.wait_ge(s["proj_ready"], GROUPS)

            def x_high(o, i):
                if i % 2 == 0:
                    act.wait_ge(s["xt_ready"], 2 * o + i // 2 + 1)
                    wait(act, s["h_ready"], 4 * o + i - 2)
                    act.activation(xh[:, i // 2, :], bank[i // 2][:, :], ACT.Copy, scale=XS).then_inc(s["xh_done"], 1)

            def gelu(o, i):
                act.wait_ge(s["hb_done"], 4 * o + i + 1)
                act.activation(hb[i % 4], hb[i % 4], ACT.Gelu_apprx_tanh, scale=gelu_scale[:, 0:1]).then_inc(s["gelu_done"], 1)

            pipeline(act, RT // 4, 4, [(0, x_high), (2, gelu)])

            act.wait_ge(s["rs_zero"], 1)
            act.wait_ge(s["tables_in"], 16)

            def qkv_copy(b, u):
                k = TB * b + u
                act.wait_ge(s["qkv_ready"], k + 1)
                wait(act, s["roped"], k - 3)
                wait(act, s["state_ready"], k - 7)
                sides = lambda m: m.rearrange("p (s h d) -> p s h d", s=2, h=NH)
                act.activation(raw[:, u % 4], sides(bank[0][:, 0:256])[:, :, :, 0:ROT], ACT.Copy)
                act.activation(sides(qk[:, u % 8, :])[:, :, :, ROT:HD], sides(bank[0][:, 0:256])[:, :, :, ROT:HD], ACT.Copy).then_inc(s["raw_done"], 1)
                wait(act, s["o_ready"], k - 7)
                for h in range(NH):
                    hp = slice(h * HD, (h + 1) * HD)
                    last = act.activation(vd[:, u, hp], bank[0][:, 256 + h * HD:256 + (h + 1) * HD], ACT.Identity, scale=deck[:, u, h:h + 1])
                last.then_inc(s["drained0"], 1)

            def kt_copy(b, u):
                k = TB * b + u
                act.wait_ge(s["qkt_ready"], k + 1)
                wait(act, s["o_ready"], k - 7)
                if k == 4:
                    act.wait_ge(s["mish_steps"], 8 * GROUPS + 1)
                act.activation(qkT[u], bank[1][:, 0:256], ACT.Copy).then_inc(s["drained1"], 1)

            def r_copy(b, u):
                k = TB * b + u
                act.wait_ge(s["state_ready"], k + 1)
                wait(act, s["o_ready"], k - 2)
                for h in range(NH):
                    hp = slice(h * HD, (h + 1) * HD)
                    last = act.activation(rs[hp, u % 4, hp], bank[4][hp, hp], ACT.Copy)
                last.then_inc(s["drained4"], 1)

            def yn(k):
                act.wait_ge(s["gac_ready"], k // 2 + 1)
                wait(act, s["yt_done"], k - 1)
                act.activation(yn_r[:, k % 2, :], ret_all[:, k * 512:(k + 1) * 512], ACT.Identity,
                               bias=gnc[:, k // 2:k // 2 + 1], scale=gna[:, k // 2:k // 2 + 1]).then_inc(s["yn_done"], 1)

            def z0(k):
                act.wait_ge(s["r2_ready"], k + 1)
                wait(act, s["t2_ready"], k - 1)
                for v in range(4):
                    last = act.activation(xr[:, k % 2, v, :], y2_all[:, 4 * k + v, :], ACT.Identity, bias=rb[:, k % 2, v:v + 1], scale=ra[:, k % 2, v:v + 1])
                last.then_inc(s["z0_done"], 1)

            def z_copy(k):
                act.wait_ge(s["t2_ready"], k + 1)
                wait(act, s["m1_ready"], k - 1)
                act.activation(zT[:, k % 2, :], bank[6][:, :], ACT.Identity, bias=vec[:, R_L2B:R_L2B + 1], scale=vec[:, R_L2W:R_L2W + 1]).then_inc(s["drained6"], 1)

            def ffn_gelu(k):
                act.wait_ge(s["m1_ready"], k + 1)
                wait(act, s["m2_ready"], k - 1)
                act.activation(aT[:, k % 2, :], bank[7][:, :], ACT.Gelu, bias=vec[:, R_W1B:R_W1B + 1]).then_inc(s["drained7"], 1)

            written_out(B, TB, [(0, qkv_copy), (2, kt_copy), (3, r_copy), (LAG["yn"], by_group(yn)), (LAG["z0"], by_group(z0)),
                                (LAG["z"], by_group(z_copy)), (LAG["gelu"], by_group(ffn_gelu))])

        @block.gpsimd
        def _(pool):
            pool.memset(zeros[:, :], 0.0).then_inc(s["zero_in"], 1)
            pool.memset(rs[:, :, :], 0.0).then_inc(s["rs_zero"], 1)
            pool.wait_ge(s["cst_in"], 16)
            chain = [0]

            def link(ins):
                chain[0] += 1
                ins.then_inc(s["link_p"], 1)
                pool.wait_ge(s["link_p"], chain[0])

            def rsqrt(k):
                pool.wait_ge(s["ve_ready"], k + 1)
                pool.tensor_tensor(ra[:, k, :], ve[:, k, :], C["mhalf"][:, 0:4], ALU.pow).then_inc(s["r_ready"], 1)

            groups([(0, rsqrt)])
            pool.wait_ge(s["r_ready"], GROUPS)
            flat = lambda m: m[:, :, :].rearrange("p k u -> p (k u)")
            link(pool.tensor_tensor(rb[:, :, :], mv[:, :, :, 1], ra[:, :, :], ALU.mult))
            link(pool.tensor_tensor(flat(rb), flat(rb), flat(ra), ALU.mult))
            link(pool.tensor_tensor(flat(rc), flat(rb), C["eps"], ALU.add))
            pool.tensor_tensor(flat(rb), flat(rc), C["mhalf"], ALU.pow).then_inc(s["r2n_ready"], 1)

            pool.wait_ge(s["idx_ready"], 1)
            pool.wait_ge(s["zeroed"], 16)
            for idx in (idx1, idx2):
                if idx is idx2:
                    pool.wait_ge(s["idx_ready"], 2)
                for t in range(TILES):
                    pool.indirect_dma_start(out=slots_x, out_offset=bass.IndirectOffsetOnAxis(ap=idx[:, t:t + 1], axis=0),
                                            in_=xn_all[:, t, :], in_offset=None).then_inc(s["scattered"], 16)

            def gather(b, u):
                t = TB * b + u
                wait(pool, s["combined"], t - 3)
                for j, idx in enumerate((idx1, idx2)):
                    pool.indirect_dma_start(out=yg[:, t % 4, j, :], out_offset=None, in_=slots_y,
                                            in_offset=bass.IndirectOffsetOnAxis(ap=idx[:, t:t + 1], axis=0)).then_inc(s[f"gath{t % 4}"], 16)

            def group_rsqrt(b):
                pool.wait_ge(s["gve_ready"], b + 1)
                pool.tensor_tensor(gvb[:, b:b + 1], gva[:, b:b + 1], C["mhalf"][:, 0:1], ALU.pow).then_inc(s["gr_ready"], 1)

            def y_mul(k):
                pool.wait_ge(s["yn_done"], k + 1)
                wait(pool, s["wo_ready"], k - 1)
                pool.tensor_tensor(yT[:, k % 2, :], yn_r[:, k % 2, :], gate_all[:, k * 512:(k + 1) * 512], ALU.mult).then_inc(s["yt_done"], 1)

            def second_rsqrt(k):
                pool.wait_ge(s["ve2_ready"], k + 1)
                wait(pool, s["z0_done"], k - 1)
                pool.tensor_tensor(ra[:, k % 2, :], ve[:, k % 2, :], C["mhalf"][:, 0:4], ALU.pow).then_inc(s["pow2"], 1)
                pool.wait_ge(s["pow2"], k + 1)
                pool.tensor_tensor(rb[:, k % 2, :], ra[:, k % 2, :], negm[:, k % 2, :], ALU.mult).then_inc(s["r2_ready"], 1)

            def add_y2(k):
                pool.wait_ge(s["ve2_ready"], k + 1)
                pool.wait_ge(s["combined"], 4 * k + 4)
                x4 = x_all[:, 4 * k:4 * k + 4, :]
                pool.tensor_tensor(x4, x4, y2_all[:, 4 * k:4 * k + 4, :], ALU.add).then_inc(s["xy_done"], 1)

            for i in range(2):
                pool.wait_ge(s[f"st_done{i}"], 16 * BLOCKS // 2)
            written_out(B, TB, [(LAG["rsqrt"], by_sequence(group_rsqrt)), (LAG["y_mul"], by_group(y_mul)), (LAG["second"], by_group(second_rsqrt)),
                                (LAG["second"], by_group(add_y2)), (0, gather)])

        @block.vector
        def _(dve):
            chain = [0]

            def link(ins):
                chain[0] += 1
                ins.then_inc(s["link_v"], 1)
                dve.wait_ge(s["link_v"], chain[0])

            def moments(x4, i, k, stat, aggr, ready):
                for u in range(4):
                    last = dve.bn_stats(stats[:, i, u, :], x4(u))
                last.then_inc(s[stat], 1)
                dve.wait_ge(s[stat], k + 1)
                for u in range(4):
                    last = dve.bn_aggr(mv[:, i, u, :], stats[:, i, u, :])
                last.then_inc(s[aggr], 1)
                dve.wait_ge(s[aggr], k + 1)
                dve.tensor_scalar(ve[:, i, :], mv[:, i, :, 1], EPS, None, ALU.add).then_inc(s[ready], 1)

            def p1_moments(k):
                dve.wait_ge(s[f"x_in{k}"], 16)
                moments(lambda u: x_all[:, 4 * k + u, :], k, k, "st1", "ag1", "ve_ready")

            def p1_norm(k):
                dve.wait_ge(s["r_ready"], k + 1)
                for u in range(4):
                    last = dve.tensor_scalar(xn_all[:, 4 * k + u, :], x_all[:, 4 * k + u, :], mv[:, k, u, 0:1], ra[:, k, u:u + 1], ALU.subtract, ALU.mult)
                last.then_inc(s["xn_done"], 1)

            groups([(0, p1_moments), (1, p1_norm)])

            em8 = C["em8"].unsqueeze(1).broadcast_to([P, TILES, E])
            wide = lambda m: m[:, :].unsqueeze(2).broadcast_to([P, TILES, E])
            by_e = lambda m: m.rearrange("p t e -> p e t")
            dve.wait_ge(s["lg_ready"], GROUPS)
            lg = bank[4][:, 0:256].rearrange("p (t e) -> p t e", e=E)
            for m, oh in ((m1, oh1), (m2, oh2)):
                src = lg if m is m1 else tb[:, :, :]
                link(dve.tensor_reduce(m[:, :], src, AX.X, ALU.max))
                link(dve.tensor_tensor(ta[:, :, :], src, wide(m), ALU.is_equal))
                link(dve.tensor_tensor(ta[:, :, :], ta[:, :, :], em8, ALU.mult))
                link(dve.tensor_reduce(im[:, :], ta[:, :, :], AX.X, ALU.min))
                link(dve.tensor_tensor(oh[:, :, :], em8, wide(im), ALU.is_equal))
                if m is m1:
                    link(dve.scalar_tensor_tensor(tb[:, :, :], oh[:, :, :], -3e38, lg, ALU.mult, ALU.add))
            dve.tensor_tensor(ta[:, :, :], oh1[:, :, :], oh2[:, :, :], ALU.add).then_inc(s["mask_ready"], 1)
            dve.tensor_tensor(dd[:, :], m2[:, :], m1[:, :], ALU.subtract).then_inc(s["dd_ready"], 1)
            dve.wait_ge(s["rank_ready"], 1)
            link(dve.tensor_copy(tot[:, :, :], by_e(bank[6][:, 0:256].rearrange("p (t e) -> p t e", e=E))))
            flat = lambda m: m[:, :, :].rearrange("p e t -> p (e t)")
            link(dve.tensor_tensor_scan(flat(cum), C["ones"], flat(tot), 0.0, ALU.mult, ALU.add))
            link(dve.tensor_copy(cnt[:, :], cum[:, :, TILES - 1]))
            link(dve.tensor_tensor(pad[:, 1:E], cnt[:, 1:E], cnt[:, 0:E - 1], ALU.subtract))
            link(dve.tensor_copy(pad[:, 0:1], cnt[:, 0:1]))
            link(dve.tensor_scalar(cnti[:, :], pad[:, :], float(SW - 1), None, ALU.add))
            link(dve.tensor_scalar(cnti[:, :], cnti[:, :], 8, 8, ALU.logical_shift_right, ALU.logical_shift_left))
            link(dve.tensor_tensor(adj[:, :], cnt[:, :], pad[:, :], ALU.subtract))
            link(dve.tensor_copy(pad[:, :], cnti[:, :]))
            link(dve.tensor_tensor_scan(endp[:, :], C["ones"][:, 0:E], pad[:, :], 0.0, ALU.mult, ALU.add))
            link(dve.tensor_tensor(pad[:, :], endp[:, :], pad[:, :], ALU.subtract))
            link(dve.tensor_tensor(adj[:, :], pad[:, :], adj[:, :], ALU.subtract))
            link(dve.tensor_tensor(posn[:, :, :], cum[:, :, :], tot[:, :, :], ALU.subtract))
            link(dve.tensor_tensor(posn[:, :, :], posn[:, :, :], adj[:, :].unsqueeze(2).broadcast_to([P, E, TILES]), ALU.add))
            link(dve.tensor_tensor(posn[:, :, :], posn[:, :, :], by_e(bank[6][:, 256:512].rearrange("p (t e) -> p t e", e=E)), ALU.add))
            for oh, idx in ((oh1, idx1), (oh2, idx2)):
                link(dve.tensor_tensor(tb[:, :, :], oh[:, :, :], posn[:, :, :].rearrange("p e t -> p t e"), ALU.mult))
                link(dve.tensor_reduce(im[:, :], tb[:, :, :], AX.X, ALU.add))
                dve.tensor_copy(idx[:, :], im[:, :]).then_inc(s["idx_ready"], 1)
                dve.wait_ge(s["idx_ready"], 1 if idx is idx1 else 2)
            link(dve.tensor_tensor(ended[:, :, :], C["slot"][0:1, :].unsqueeze(2).broadcast_to([1, RT, E]), endp[0:1, :].unsqueeze(1).broadcast_to([1, RT, E]), ALU.is_ge))
            link(dve.tensor_reduce(tile_e[:, :], ended[:, :, :], AX.X, ALU.add))
            link(dve.tensor_scalar(tile_e[:, :], tile_e[:, :], float(E - 1), None, ALU.min))
            link(dve.tensor_scalar(off_b[:, :], tile_e[:, :], float(HC), None, ALU.mult))
            link(dve.tensor_scalar(off_y[:, :], tile_e[:, :], float(D), None, ALU.mult))
            dve.tensor_scalar(off_w[:, :], tile_e[:, :], float(HID), None, ALU.mult).then_inc(s["temps_free"], 1)
            dve.wait_ge(s["temps_free"], 1)
            dve.sem_inc(s["off_ready"], 1)
            dve.wait_ge(s["ex_ready"], 1)
            link(dve.tensor_scalar(g1[:, :], g2[:, :], 1.0, None, ALU.add))
            link(dve.reciprocal(g1[:, :], g1[:, :]))
            link(dve.tensor_tensor(g2[:, :], g2[:, :], g1[:, :], ALU.mult))

            def acc(k):
                x4 = x_all[:, 4 * k:4 * k + 4, :]
                dve.wait_ge(s["proj_ready"], k + 1)
                dve.tensor_tensor(x4, x4, bank[7][:, :].rearrange("p (t d) -> p t d", t=4), ALU.add).then_inc(s["acc_done"], 1)
                dve.wait_ge(s["acc_done"], k + 1)
                dve.tensor_tensor(x4, x4, out_bias[:, :].unsqueeze(1).broadcast_to([P, 4, D]), ALU.add).then_inc(s["bias_done"], 1)

            def gate_out(k):
                dve.wait_ge(s["g_ready"], k + 1)
                dve.tensor_copy(gate_all[:, k * 512:(k + 1) * 512], bank[4][:, :]).then_inc(s["g_kept"], 1)
                dve.tensor_scalar(xnT[:, k * 512:(k + 1) * 512], bank[4][:, :], 20.0, None, ALU.min).then_inc(s["clamped"], 1)

            def scale_steps(k):
                if k == 0:
                    dve.wait_ge(s["wexp_in"], 16)
                    dve.tensor_reduce(amax[:, :], wfc32, AX.X, ALU.max, apply_absolute_value=True).then_inc(s["amax_ready"], 1)
                if k == 1:
                    dve.wait_ge(s["amaxt_ready"], 1)
                    dve.tensor_reduce(amax_row[:, :], bank[6][0:1, 0:P], AX.X, ALU.max).then_inc(s["arow_ready"], 1)
                if k == 2:
                    dve.wait_ge(s["abc_ready"], 1)
                    link(dve.tensor_scalar(amax[:, :], bank[6][:, 0:1], 2.0 ** -40, None, ALU.max))
                    link(dve.tensor_scalar(exponent[:, :], amax[:, :].bitcast(I32), 23, None, ALU.logical_shift_right))
                    link(dve.tensor_scalar(scale[:, :].bitcast(I32), exponent[:, :], -1, 2 * 127 + TOP, ALU.mult, ALU.add))
                    link(dve.tensor_scalar(inverse[:, :].bitcast(I32), exponent[:, :], -TOP, None, ALU.add))
                    link(dve.tensor_scalar(scale[:, :].bitcast(I32), scale[:, :].bitcast(I32), 23, None, ALU.logical_shift_left))
                    link(dve.tensor_scalar(inverse[:, :].bitcast(I32), inverse[:, :].bitcast(I32), 23, None, ALU.logical_shift_left))
                    link(dve.tensor_scalar(bias16[:, :], vec[:, R_FC:R_FC + E * HC], scale[:, 0:1], XS, ALU.mult, ALU.mult))
                    dve.tensor_scalar(gelu_scale[:, :], inverse[:, 0:1], 1.0 / XS, None, ALU.mult).then_inc(s["scale_ready"], 1)
                if k >= 4:
                    part = slice((k - 4) * 1024, (k - 3) * 1024)
                    dve.wait_ge(s["high_done"], k - 3)
                    dve.scalar_tensor_tensor(wfc16[:, 1, part], wfc32[:, part], scale[:, 0:1], wfc16[:, 0, part], ALU.mult, ALU.subtract).then_inc(s["low_done"], 1)

            dve.wait_ge(s["pre_act"], 1)
            groups([(1, gate_out), (1, acc), (1, scale_steps)])
            dve.wait_ge(s["bias_done"], GROUPS)
            dve.wait_ge(s["low_done"], 4)
            dve.sem_inc(s["split_done"], 1)

            def x_low(o, i):
                if i % 2 == 0:
                    dve.wait_ge(s["xh_done"], 2 * o + i // 2 + 1)
                    dve.scalar_tensor_tensor(xl[:, i // 2, :], bank[i // 2][:, :], XS, xh[:, i // 2, :], ALU.mult, ALU.subtract).then_inc(s["xl_done"], 1)

            def add_bias(o, i):
                k = 4 * o + i
                e = dve.value_load(off_b[0:1, bass.ds(k, 1)], min_val=0, max_val=(E - 1) * HC)
                dve.wait_ge(s["h_ready"], k + 1)
                wait(dve, s["y_ready"], k - 3)
                c4 = lambda m: m.rearrange("p (c n) -> p c n", c=HC)
                dve.tensor_tensor(c4(hb[i % 4]), c4(pairs[i % 2][:, :, :].rearrange("p b n -> p (b n)")),
                                  bias16[:, bass.ds(e, HC)].unsqueeze(2).broadcast_to([P, HC, SW]), ALU.add).then_inc(s["hb_done"], 1)

            def y_out(o, i):
                k = 4 * o + i
                e = dve.value_load(off_y[0:1, bass.ds(k, 1)], min_val=0, max_val=(E - 1) * D)
                dve.wait_ge(s["y_ready"], k + 1)
                if i % 2 == 0:
                    wait(dve, s[f"st_done{i // 2}"], 16 * o)
                dve.tensor_tensor(ys[:, i // 2, i % 2 * 2:i % 2 * 2 + 2, :], bank[6 + i % 2][:, 0:SW].rearrange("p (v d) -> p v d", v=2),
                                  bproj[:, bass.ds(e, D)].unsqueeze(1).broadcast_to([P, 2, D]), ALU.add).then_inc(s["ys_done"], 1)

            def mish(o, i):
                if isinstance(o, int) and o < RT // 4 - GROUPS:
                    return
                k = o - (RT // 4 - GROUPS)
                n, g, r = xnT[:, bass.ds(512 * k, 512)], gate_all[:, bass.ds(512 * k, 512)], tr[:, 0, :]
                for j in (2 * i, 2 * i + 1):
                    part = tr[:, 0, (j - 2) % 4 * P:((j - 2) % 4 + 1) * P]
                    f = (
                        lambda: dve.scalar_tensor_tensor(n, n, 2.0, n, ALU.add, ALU.mult),
                        lambda: dve.tensor_scalar(r, n, 2.0, None, ALU.add),
                        *[lambda: dve.reciprocal(part, part)] * 4,
                        lambda: dve.tensor_tensor(n, n, r, ALU.mult),
                        lambda: dve.tensor_tensor(g, g, n, ALU.mult),
                    )[j]
                    dve.wait_ge(s["mish_steps"], 8 * k + j + 1)
                    f().then_inc(s["mish_steps"], 1)

            dve.wait_ge(s["mish_exp"], 1)
            dve.sem_inc(s["mish_steps"], 1)
            dve.wait_ge(s["watt_in"], 16 * 5)
            pipeline(dve, RT // 4, 4, [(0, x_low), (2, add_bias), (4, y_out), (0, mish)])

            def rope(b, u):
                k = TB * b + u
                dve.wait_ge(s["raw_done"], k + 1)
                src = raw[:, u % 4]
                rt1, rt2 = rt1_r[:, u % 2], rt2_r[:, u % 2]
                wait(dve, s["roped"], k - 1)
                over = lambda m, n: m.unsqueeze(2).broadcast_to([P, 2, NH, n])
                dve.tensor_tensor(rt1[:, :, :, :], src, over(ropec[:, u, :, :], ROT), ALU.mult)
                dve.tensor_tensor(rt2[:, :, :, 0::2], src[:, :, :, 1:ROT:2], over(ropes[:, u, :, 0::2], ROT // 2), ALU.mult)
                dve.tensor_tensor(rt2[:, :, :, 1::2], src[:, :, :, 0:ROT:2], over(ropes[:, u, :, 1::2], ROT // 2), ALU.mult).then_inc(s["rot_parts"], 1)

            def rope_sum(b, u):
                k = TB * b + u
                dve.wait_ge(s["rot_parts"], k + 1)
                dve.tensor_tensor(qk[:, u % 8, :].rearrange("p (s h d) -> p s h d", s=2, h=NH)[:, :, :, 0:ROT],
                                  rt1_r[:, u % 2], rt2_r[:, u % 2], ALU.add).then_inc(s["roped"], 1)

            def mask(b, u):
                k = TB * b + u
                dve.wait_ge(s["st_ready"], k + 1)
                wait(dve, s["o_ready"], k - 3)
                dve.tensor_tensor(stm[:, u % 4, :, :], pair[:, :, 0:P],
                                  C["causal"].unsqueeze(1).broadcast_to([P, NH, P]), ALU.mult).then_inc(s["drained2"], 1)

            def ret_out(b, u):
                k = TB * b + u
                dve.wait_ge(s["o_ready"], k + 1)
                dve.tensor_tensor(ret_all[:, k * P:(k + 1) * P], bank[5][:, 0:P], decq[:, u, :], ALU.mult).then_inc(s["drained5"], 1)

            def combine_first(b, u):
                k = TB * b + u
                dve.wait_ge(s[f"gath{u % 4}"], 32 * (2 * b + u // 4 + 1))
                dve.scalar_tensor_tensor(x_all[:, k, :], yg[:, u % 4, 0, :], g1[:, k:k + 1], x_all[:, k, :], ALU.mult, ALU.add).then_inc(s["part_sums"], 1)

            def combine_second(b, u):
                k = TB * b + u
                dve.wait_ge(s["part_sums"], k + 1)
                dve.scalar_tensor_tensor(x_all[:, k, :], yg[:, u % 4, 1, :], g2[:, k:k + 1], x_all[:, k, :], ALU.mult, ALU.add).then_inc(s["combined"], 1)

            def norm_moments(b, u):
                if u % 4 == 3:
                    g = 2 * b + u // 4
                    dve.wait_ge(s["drained5"], 4 * g + 4)
                    dve.bn_stats(gst[:, b, u // 4, :], ret_all[:, g * 512:(g + 1) * 512]).then_inc(s["gst_done"], 1)
                if u == TB - 1:
                    dve.wait_ge(s["gst_done"], 2 * b + 2)
                    dve.bn_aggr(gmv[:, b, :], gst[:, b, :, :]).then_inc(s["gsum_ready"], 1)

            def norm_mean(b):
                dve.wait_ge(s["gtot_ready"], b + 1)
                dve.tensor_scalar(gnm[:, b:b + 1], bank[6][:, 0:1], -1.0 / HD, None, ALU.mult).then_inc(s["gmean_ready"], 1)
                dve.wait_ge(s["gmean_ready"], b + 1)
                dve.sem_inc(s["drained6"], 1)
                link(dve.tensor_tensor(gdev[:, b:b + 1], gmv[:, b, 0:1], gnm[:, b:b + 1], ALU.add))
                dve.scalar_tensor_tensor(gsq[:, b:b + 1], gdev[:, b:b + 1], gdev[:, b:b + 1], gmv[:, b, 1:2], ALU.mult, ALU.add).then_inc(s["gsq_ready"], 1)

            def norm_var(b):
                dve.wait_ge(s["gtot2_ready"], b + 1)
                dve.tensor_scalar(gva[:, b:b + 1], bank[6][:, 0:1], 1.0 / HD, EPS, ALU.mult, ALU.add).then_inc(s["gve_ready"], 1)
                dve.wait_ge(s["gve_ready"], b + 1)
                dve.sem_inc(s["drained6"], 1)

            def norm_scale(b):
                dve.wait_ge(s["gr_ready"], b + 1)
                dve.tensor_tensor(gna[:, b:b + 1], gvb[:, b:b + 1], gn[:, 0:1], ALU.mult).then_inc(s["gna_ready"], 1)
                dve.wait_ge(s["gna_ready"], b + 1)
                dve.scalar_tensor_tensor(gnc[:, b:b + 1], gnm[:, b:b + 1], gna[:, b:b + 1], gn[:, 1:2], ALU.mult, ALU.add).then_inc(s["gac_ready"], 1)

            def y2(k):
                y4 = y2_all[:, 4 * k:4 * k + 4, :]
                dve.wait_ge(s["wo_ready"], k + 1)
                dve.tensor_tensor(y4, bank[6][:, :].rearrange("p (t d) -> p t d", t=4), xn_all[:, 4 * k:4 * k + 4, :], ALU.add).then_inc(s["drained6"], 1)
                dve.wait_ge(s["drained6"], 6 * (k // 2) + 3 + k % 2)
                wait(dve, s["z0_done"], k - 1)
                moments(lambda v: y2_all[:, 4 * k + v, :], k % 2, k, "st2", "ag2", "negm_ready")
                dve.tensor_scalar(negm[:, k % 2, :], mv[:, k % 2, :, 0], -1.0, None, ALU.mult).then_inc(s["ve2_ready"], 1)

            def final(k):
                dve.wait_ge(s["m2_ready"], k + 1)
                wait(dve, s[f"out_done{k % 2}"], 16 * (k // 2))
                dve.wait_ge(s["xy_done"], k + 1)
                dve.tensor_tensor(ob[:, k % 2, :, :], bank[7][:, :].rearrange("p (t d) -> p t d", t=4), x_all[:, 4 * k:4 * k + 4, :], ALU.add).then_inc(s["fin_ready"], 1)
                dve.wait_ge(s["fin_ready"], k + 1)
                dve.sem_inc(s["drained7"], 1)

            dve.wait_ge(s["tables_in"], 16)
            written_out(B, TB, [(1, rope), (6, ret_out), (1, rope_sum), (4, mask), (4, combine_first), (4, combine_second), (7, norm_moments),
                                (LAG["mean"], by_sequence(norm_mean)), (LAG["var"], by_sequence(norm_var)), (LAG["scale"], by_sequence(norm_scale)),
                                (LAG["y2"], by_group(y2)), (LAG["final"], by_group(final))])


_INS = ["L0_attn_x", "L0_attn_ln1_w", "L0_attn_ln1_b", "L0_attn_wqkv_w", "L0_attn_wg_w", "L0_attn_wo_w", "L0_attn_gn_w", "L0_attn_gn_b",
        "L0_attn_ln2_w", "L0_attn_ln2_b", "L0_attn_w1_w", "L0_attn_w1_b", "L0_attn_w2_w", "L0_attn_w2_b", "L0_ffn_Wfc_s", "L0_ffn_bfc_s",
        "L0_ffn_Wproj_s", "L0_ffn_bproj_s", "L0_ffn_Wr", "L0_ffn_Wfc", "L0_ffn_bfc", "L0_ffn_Wproj", "L0_ffn_bproj"]


def kernel(**inputs):
    import concourse.bacc as bacc
    from concourse.bass_utils import run_bass_kernel_spmd

    nc = bacc.Bacc("TRN2", target_bir_lowering=False, num_devices=1)
    arrays, args = {}, {}
    for name in _INS:
        arrays[name] = np.ascontiguousarray(inputs[name])
        args[name] = nc.dram_tensor(name, arrays[name].shape, F32, kind="ExternalInput").ap()
    parts, cols, at = constants(), {}, 0
    for name, v in parts.items():
        cols[name] = (at, at + v.shape[1])
        at += v.shape[1]
    arrays["const"] = np.ascontiguousarray(np.concatenate(list(parts.values()), axis=1).astype(np.float32))
    const = nc.dram_tensor("const", arrays["const"].shape, F32, kind="ExternalInput").ap()
    out = nc.dram_tensor("out", (B, S, D), F32, kind="ExternalOutput").ap()
    build(nc, args, const, cols, out)
    return run_bass_kernel_spmd(nc, [arrays], core_ids=[0]).results[0]["out"]
```
